# Optimizing a Trainium2 kernel written in Bass

```python
import numpy as np
import jax
import jax.numpy as jnp

def _softmax(x, axis=-1):
    return jax.nn.softmax(x, axis=axis)

def _gelu(x):
    return jax.nn.gelu(x, approximate=True)

def _silu(x):
    return jax.nn.silu(x)

def _sigmoid(x):
    return jax.nn.sigmoid(x)

def _layernorm(x, axis=-1, eps=1e-05):
    m = jnp.mean(x, axis=axis, keepdims=True)
    v = jnp.var(x, axis=axis, keepdims=True)
    return (x - m) / jnp.sqrt(v + eps)

def _scatter_add(tgt, idx, src, axis=0):
    return tgt.at[idx].add(src)

def _segment_sum(src, seg, n):
    return jax.ops.segment_sum(src, seg, n)
kernel_name = 'mk_xattn_seq_d2_seqx_r4_97b3fd'

def setup_inputs(seed: int=0):
    np.random.seed(seed)
    _w = jnp.asarray

    def _rec_inputs():
        import jax
        import jax.numpy as jnp
        _rk = jax.random.key(seed)
        x = -0.0002928 + 1 * jax.random.normal(jax.random.fold_in(_rk, 1), (8, 256, 512), jnp.float32)
        _lenS = 256 - jax.random.randint(jax.random.fold_in(_rk, 7), (8,), 0, max(1, 256 // 4) + 1, jnp.int32)
        _lenS2 = 256 - jax.random.randint(jax.random.fold_in(_rk, 8), (8,), 0, max(1, 256 // 4) + 1, jnp.int32)
        _ctx_2048P = jax.random.normal(jax.random.fold_in(_rk, 11), (8, 16, 512), jnp.float32)
        _ctx_2048c = jax.random.dirichlet(jax.random.fold_in(_rk, 511), 0.3 * jnp.ones((16,), jnp.float32), (8, 256))
        _ctx_2048t = jnp.einsum('bsk,bkd->bsd', _ctx_2048c, _ctx_2048P)
        _ctx_2048t = _ctx_2048t * jax.lax.rsqrt(jnp.mean(jnp.square(_ctx_2048t)) + 1e-12) * 0.953939
        ctx_2048 = 0.000189249 + 0.0999589 * (_ctx_2048t + 0.3 * jax.random.normal(jax.random.fold_in(_rk, 611), (8, 256, 512), jnp.float32))
        _validS = jnp.arange(256)[None, :] < _lenS[:, None]
        _validS2 = jnp.arange(256)[None, :] < _lenS2[:, None]
        _causal = jnp.tril(jnp.ones((256, 256), dtype=bool))
        mask_Bx1xSxS2_ff0 = jnp.where(jnp.ones((8, 1, 256, 256), dtype=bool), 0.0, -1000000000.0).astype(jnp.float32)
        return (x, ctx_2048, mask_Bx1xSxS2_ff0)
    x, ctx_2048, mask_Bx1xSxS2_ff0 = _rec_inputs()

    def _L0_xattn_setup():
        import jax, jax.numpy as jnp
        import numpy as np
        B, L, E, H = (4, 128, 512, 32)
        S = E // H
        EXTRA_MAA, EXTRA_DECAY = (32, 64)
        EPS = 1e-05

        def _ln(x, w, b):
            m = jnp.mean(x, axis=-1, keepdims=True)
            v = jnp.mean((x - m) ** 2, axis=-1, keepdims=True)
            return (x - m) * jax.lax.rsqrt(v + EPS) * w + b

        def _token_shift(xn, prev_row):
            first = (prev_row - xn[:, 0])[:, None]
            rest = xn[:, :-1] - xn[:, 1:]
            return jnp.concatenate([first, rest], axis=1)
        key = jax.random.key(seed)
        ks = jax.random.split(key, 24)
        rn = lambda k, shp, s=1.0: jax.random.normal(k, shp, dtype=jnp.float32) * s
        return dict(x=rn(ks[0], (B, L, E)), state=rn(ks[1], (B, 2 + S, E), 0.1), ln1_w=jnp.ones((E,), jnp.float32), ln1_b=jnp.zeros((E,), jnp.float32), ln2_w=jnp.ones((E,), jnp.float32), ln2_b=jnp.zeros((E,), jnp.float32), maa_x=rn(ks[2], (E,), 0.02), maa_w1=rn(ks[3], (E, 5 * EXTRA_MAA), 0.02), maa_w2=rn(ks[4], (5, EXTRA_MAA, E), 0.02), maa_stack=rn(ks[5], (5, E), 0.02), time_decay=rn(ks[6], (E,), 0.5), decay_w1=rn(ks[7], (E, EXTRA_DECAY), 0.02), decay_w2=rn(ks[8], (EXTRA_DECAY, E), 0.02), faaaa=rn(ks[9], (H, S), 0.1), Wr=rn(ks[10], (E, E), 0.02), Wk=rn(ks[11], (E, E), 0.02), Wv=rn(ks[12], (E, E), 0.02), Wg=rn(ks[13], (E, E), 0.02), Wo=rn(ks[14], (E, E), 0.02), gn_w=jnp.ones((E,), jnp.float32), gn_b=jnp.zeros((E,), jnp.float32), ffn_maa_k=rn(ks[15], (E,), 0.02), ffn_maa_r=rn(ks[16], (E,), 0.02), ffn_Wk=rn(ks[17], (E, E), 0.02), ffn_Wr=rn(ks[18], (E, E), 0.02), ffn_Wv=rn(ks[19], (E, E), 0.02), i=0)
    _L0_xattn_all = _L0_xattn_setup()
    _L0_xattn_in = {k: v for k, v in _L0_xattn_all.items() if k in ('ln1_w', 'ln1_b', 'ln2_w', 'ln2_b', 'maa_x', 'maa_w1', 'maa_w2', 'maa_stack', 'time_decay', 'decay_w1', 'decay_w2', 'faaaa', 'Wr', 'Wk', 'Wv', 'Wg', 'Wo', 'gn_w', 'gn_b', 'ffn_maa_k', 'ffn_maa_r', 'ffn_Wk', 'ffn_Wr', 'ffn_Wv')}
    del _L0_xattn_all

    def _L1_xattn_setup():
        import jax, jax.numpy as jnp
        import numpy as np
        H = 512
        NH = 32
        KVH = 8
        HD = H // NH
        GROUPS = NH // KVH
        EPS = 1e-06
        B, L, S = (4, 256, 256)

        def _gqa_forward(hidden_state, encoder_hidden_state, encoder_attention_mask, Wq, bq, Wk, bk, Wv, bv, Wo, bo, gamma, beta):
            b, l, _ = hidden_state.shape
            s = encoder_hidden_state.shape[1]
            q = hidden_state @ Wq + bq
            k = encoder_hidden_state @ Wk + bk
            v = encoder_hidden_state @ Wv + bv
            q = q.reshape(b, l, KVH, GROUPS, HD).transpose(0, 2, 3, 1, 4)
            k = k.reshape(b, s, KVH, HD).transpose(0, 2, 1, 3)
            v = v.reshape(b, s, KVH, HD).transpose(0, 2, 1, 3)
            scale = 1.0 / jnp.sqrt(jnp.asarray(HD, q.dtype))
            scores = jnp.einsum('bkgld,bksd->bkgls', q, k) * scale
            scores = scores + encoder_attention_mask[:, :, None, :, :]
            attn = jax.nn.softmax(scores, axis=-1)
            out = jnp.einsum('bkgls,bksd->bkgld', attn, v)
            out = out.transpose(0, 3, 1, 2, 4).reshape(b, l, H)
            out = out @ Wo + bo
            x = out + hidden_state
            mu = jnp.mean(x, axis=-1, keepdims=True)
            var = jnp.var(x, axis=-1, keepdims=True)
            return (x - mu) * jax.lax.rsqrt(var + EPS) * gamma + beta
        key = jax.random.key(seed)
        ks = jax.random.split(key, 12)
        sd = 0.02
        return {'hidden_state': jax.random.normal(ks[0], (B, L, H), jnp.float32), 'encoder_hidden_state': jax.random.normal(ks[1], (B, S, H), jnp.float32), 'encoder_attention_mask': jnp.zeros((B, 1, L, S), jnp.float32), 'Wq': jax.random.normal(ks[2], (H, H), jnp.float32) * sd, 'bq': jnp.zeros((H,), jnp.float32), 'Wk': jax.random.normal(ks[3], (H, KVH * HD), jnp.float32) * sd, 'bk': jnp.zeros((KVH * HD,), jnp.float32), 'Wv': jax.random.normal(ks[4], (H, KVH * HD), jnp.float32) * sd, 'bv': jnp.zeros((KVH * HD,), jnp.float32), 'Wo': jax.random.normal(ks[5], (H, H), jnp.float32) * sd, 'bo': jnp.zeros((H,), jnp.float32), 'gamma': jnp.ones((H,), jnp.float32), 'beta': jnp.zeros((H,), jnp.float32)}
    _L1_xattn_all = _L1_xattn_setup()
    _L1_xattn_in = {k: v for k, v in _L1_xattn_all.items() if k in ('Wq', 'bq', 'Wk', 'bk', 'Wv', 'bv', 'Wo', 'bo', 'gamma', 'beta')}
    del _L1_xattn_all
    return {'x': x, 'ctx_2048': ctx_2048, 'mask_Bx1xSxS2_ff0': mask_Bx1xSxS2_ff0, 'L0_xattn_ln1_w': _L0_xattn_in['ln1_w'], 'L0_xattn_ln1_b': _L0_xattn_in['ln1_b'], 'L0_xattn_ln2_w': _L0_xattn_in['ln2_w'], 'L0_xattn_ln2_b': _L0_xattn_in['ln2_b'], 'L0_xattn_maa_x': _L0_xattn_in['maa_x'], 'L0_xattn_maa_w1': _L0_xattn_in['maa_w1'], 'L0_xattn_maa_w2': _L0_xattn_in['maa_w2'], 'L0_xattn_maa_stack': _L0_xattn_in['maa_stack'], 'L0_xattn_time_decay': _L0_xattn_in['time_decay'], 'L0_xattn_decay_w1': _L0_xattn_in['decay_w1'], 'L0_xattn_decay_w2': _L0_xattn_in['decay_w2'], 'L0_xattn_faaaa': _L0_xattn_in['faaaa'], 'L0_xattn_Wr': _L0_xattn_in['Wr'], 'L0_xattn_Wk': _L0_xattn_in['Wk'], 'L0_xattn_Wv': _L0_xattn_in['Wv'], 'L0_xattn_Wg': _L0_xattn_in['Wg'], 'L0_xattn_Wo': _L0_xattn_in['Wo'], 'L0_xattn_gn_w': _L0_xattn_in['gn_w'], 'L0_xattn_gn_b': _L0_xattn_in['gn_b'], 'L0_xattn_ffn_maa_k': _L0_xattn_in['ffn_maa_k'], 'L0_xattn_ffn_maa_r': _L0_xattn_in['ffn_maa_r'], 'L0_xattn_ffn_Wk': _L0_xattn_in['ffn_Wk'], 'L0_xattn_ffn_Wr': _L0_xattn_in['ffn_Wr'], 'L0_xattn_ffn_Wv': _L0_xattn_in['ffn_Wv'], 'L1_xattn_Wq': _L1_xattn_in['Wq'], 'L1_xattn_bq': _L1_xattn_in['bq'], 'L1_xattn_Wk': _L1_xattn_in['Wk'], 'L1_xattn_bk': _L1_xattn_in['bk'], 'L1_xattn_Wv': _L1_xattn_in['Wv'], 'L1_xattn_bv': _L1_xattn_in['bv'], 'L1_xattn_Wo': _L1_xattn_in['Wo'], 'L1_xattn_bo': _L1_xattn_in['bo'], 'L1_xattn_gamma': _L1_xattn_in['gamma'], 'L1_xattn_beta': _L1_xattn_in['beta']}

def reference(x, ctx_2048, mask_Bx1xSxS2_ff0, L0_xattn_ln1_w, L0_xattn_ln1_b, L0_xattn_ln2_w, L0_xattn_ln2_b, L0_xattn_maa_x, L0_xattn_maa_w1, L0_xattn_maa_w2, L0_xattn_maa_stack, L0_xattn_time_decay, L0_xattn_decay_w1, L0_xattn_decay_w2, L0_xattn_faaaa, L0_xattn_Wr, L0_xattn_Wk, L0_xattn_Wv, L0_xattn_Wg, L0_xattn_Wo, L0_xattn_gn_w, L0_xattn_gn_b, L0_xattn_ffn_maa_k, L0_xattn_ffn_maa_r, L0_xattn_ffn_Wk, L0_xattn_ffn_Wr, L0_xattn_ffn_Wv, L1_xattn_Wq, L1_xattn_bq, L1_xattn_Wk, L1_xattn_bk, L1_xattn_Wv, L1_xattn_bv, L1_xattn_Wo, L1_xattn_bo, L1_xattn_gamma, L1_xattn_beta):
    import jax
    import jax.numpy as jnp

    def _L0_xattn_ref(x, state, ln1_w, ln1_b, ln2_w, ln2_b, maa_x, maa_w1, maa_w2, maa_stack, time_decay, decay_w1, decay_w2, faaaa, Wr, Wk, Wv, Wg, Wo, gn_w, gn_b, ffn_maa_k, ffn_maa_r, ffn_Wk, ffn_Wr, ffn_Wv, i):
        import jax, jax.numpy as jnp
        import numpy as np
        B, L, E, H = (4, 128, 512, 32)
        S = E // H
        EXTRA_MAA, EXTRA_DECAY = (32, 64)
        EPS = 1e-05

        def _ln(x, w, b):
            m = jnp.mean(x, axis=-1, keepdims=True)
            v = jnp.mean((x - m) ** 2, axis=-1, keepdims=True)
            return (x - m) * jax.lax.rsqrt(v + EPS) * w + b

        def _token_shift(xn, prev_row):
            first = (prev_row - xn[:, 0])[:, None]
            rest = xn[:, :-1] - xn[:, 1:]
            return jnp.concatenate([first, rest], axis=1)
        b, l = (x.shape[0], x.shape[1])
        i0 = (2 + S) * i + 0
        i1 = (2 + S) * i + 1
        xn = _ln(x, ln1_w, ln1_b)
        sx = _token_shift(xn, state[:, i1])
        xxx = jnp.tanh((xn + sx * maa_x) @ maa_w1).reshape(b, l, 5, 1, EXTRA_MAA)
        xxx = jnp.matmul(xxx, maa_w2).reshape(b, l, 5, E)
        x5 = xn[:, :, None] + sx[:, :, None] * (maa_stack + xxx)
        w = jnp.exp(-jnp.exp(time_decay + jnp.tanh(x5[:, :, 1] @ decay_w1) @ decay_w2))
        w = w.reshape(b, l, H, S)
        r = (x5[:, :, 3] @ Wr.T).reshape(b, l, H, S)
        k = (x5[:, :, 0] @ Wk.T).reshape(b, l, H, S)
        v = (x5[:, :, 2] @ Wv.T).reshape(b, l, H, S)
        g = jax.nn.silu(x5[:, :, 4] @ Wg.T)
        s0 = state[:, (2 + S) * i + 2:(2 + S) * (i + 1)].reshape(b, H, S, S)
        u = faaaa[None, :, :, None]

        def step(s, rkvw):
            r_t, k_t, v_t, w_t = rkvw
            a = k_t[:, :, :, None] * v_t[:, :, None, :]
            out = jnp.einsum('bhk,bhkd->bhd', r_t, u * a + s)
            return (a + w_t[:, :, :, None] * s, out)
        xs = tuple((jnp.moveaxis(t, 1, 0) for t in (r, k, v, w)))
        _, outs = jax.lax.scan(step, s0, xs)
        att = jnp.moveaxis(outs, 0, 1).reshape(b, l, E)
        a4 = att.reshape(b, l, H, S)
        m = jnp.mean(a4, axis=-1, keepdims=True)
        var = jnp.mean((a4 - m) ** 2, axis=-1, keepdims=True)
        att = ((a4 - m) * jax.lax.rsqrt(var + EPS)).reshape(b, l, E) * gn_w + gn_b
        x = x + att * g @ Wo.T
        xn2 = _ln(x, ln2_w, ln2_b)
        sx2 = _token_shift(xn2, state[:, i0])
        xk = xn2 + sx2 * ffn_maa_k
        xr = xn2 + sx2 * ffn_maa_r
        rr = jax.nn.sigmoid(xr @ ffn_Wr.T)
        kk = jnp.square(jax.nn.relu(xk @ ffn_Wk.T))
        x = x + rr * (kk @ ffn_Wv.T)
        return x

    def _L1_xattn_ref(hidden_state, encoder_hidden_state, encoder_attention_mask, Wq, bq, Wk, bk, Wv, bv, Wo, bo, gamma, beta):
        import jax, jax.numpy as jnp
        import numpy as np
        H = 512
        NH = 32
        KVH = 8
        HD = H // NH
        GROUPS = NH // KVH
        EPS = 1e-06
        B, L, S = (4, 256, 256)

        def _gqa_forward(hidden_state, encoder_hidden_state, encoder_attention_mask, Wq, bq, Wk, bk, Wv, bv, Wo, bo, gamma, beta):
            b, l, _ = hidden_state.shape
            s = encoder_hidden_state.shape[1]
            q = hidden_state @ Wq + bq
            k = encoder_hidden_state @ Wk + bk
            v = encoder_hidden_state @ Wv + bv
            q = q.reshape(b, l, KVH, GROUPS, HD).transpose(0, 2, 3, 1, 4)
            k = k.reshape(b, s, KVH, HD).transpose(0, 2, 1, 3)
            v = v.reshape(b, s, KVH, HD).transpose(0, 2, 1, 3)
            scale = 1.0 / jnp.sqrt(jnp.asarray(HD, q.dtype))
            scores = jnp.einsum('bkgld,bksd->bkgls', q, k) * scale
            scores = scores + encoder_attention_mask[:, :, None, :, :]
            attn = jax.nn.softmax(scores, axis=-1)
            out = jnp.einsum('bkgls,bksd->bkgld', attn, v)
            out = out.transpose(0, 3, 1, 2, 4).reshape(b, l, H)
            out = out @ Wo + bo
            x = out + hidden_state
            mu = jnp.mean(x, axis=-1, keepdims=True)
            var = jnp.var(x, axis=-1, keepdims=True)
            return (x - mu) * jax.lax.rsqrt(var + EPS) * gamma + beta
        return _gqa_forward(hidden_state, encoder_hidden_state, encoder_attention_mask, Wq, bq, Wk, bk, Wv, bv, Wo, bo, gamma, beta)
    x = _L0_xattn_ref(x, ctx_2048, L0_xattn_ln1_w, L0_xattn_ln1_b, L0_xattn_ln2_w, L0_xattn_ln2_b, L0_xattn_maa_x, L0_xattn_maa_w1, L0_xattn_maa_w2, L0_xattn_maa_stack, L0_xattn_time_decay, L0_xattn_decay_w1, L0_xattn_decay_w2, L0_xattn_faaaa, L0_xattn_Wr, L0_xattn_Wk, L0_xattn_Wv, L0_xattn_Wg, L0_xattn_Wo, L0_xattn_gn_w, L0_xattn_gn_b, L0_xattn_ffn_maa_k, L0_xattn_ffn_maa_r, L0_xattn_ffn_Wk, L0_xattn_ffn_Wr, L0_xattn_ffn_Wv, 0)
    x = _L1_xattn_ref(x, ctx_2048, mask_Bx1xSxS2_ff0, L1_xattn_Wq, L1_xattn_bq, L1_xattn_Wk, L1_xattn_bk, L1_xattn_Wv, L1_xattn_bv, L1_xattn_Wo, L1_xattn_bo, L1_xattn_gamma, L1_xattn_beta)
    return x

_drawn_inputs = setup_inputs


def setup_inputs(seed=0):
    import zlib

    import numpy as np

    out = dict(_drawn_inputs(seed))
    spreads = {'L0_xattn_ln1_w': (1.0, 0.2),
     'L0_xattn_ln1_b': (0.0, 0.1),
     'L0_xattn_ln2_w': (1.0, 0.6),
     'L0_xattn_ln2_b': (0.0, 0.8),
     'L0_xattn_gn_w': (1.0, 0.6),
     'L0_xattn_gn_b': (0.0, 0.683),
     'L1_xattn_bq': (0.0, 0.8),
     'L1_xattn_bk': (0.0, 0.8),
     'L1_xattn_bv': (0.0, 0.1),
     'L1_xattn_bo': (0.0, 0.1),
     'L1_xattn_gamma': (1.0, 0.2),
     'L1_xattn_beta': (0.0, 0.1)}
    factors = {'ctx_2048': 4.757,
     'L0_xattn_maa_x': 8.0,
     'L0_xattn_maa_w1': 2.906,
     'L0_xattn_maa_w2': 2.928,
     'L0_xattn_maa_stack': 6.392,
     'L0_xattn_decay_w1': 8.0,
     'L0_xattn_decay_w2': 8.0,
     'L0_xattn_faaaa': 3.005,
     'L0_xattn_ffn_maa_k': 8.0,
     'L0_xattn_ffn_maa_r': 8.0,
     'L0_xattn_ffn_Wr': 4.163,
     'L1_xattn_Wq': 8.0,
     'L1_xattn_Wk': 8.0,
     'L1_xattn_Wv': 5.47}
    for name, (base, spread) in spreads.items():
        noise = np.random.default_rng([zlib.crc32(name.encode()), seed]).standard_normal(out[name].shape)
        drawn = base * np.exp(spread * noise) if base else spread * noise
        out[name] = jnp.asarray(drawn.astype(out[name].dtype))
    for name, factor in factors.items():
        out[name] = (out[name] * factor).astype(out[name].dtype)
    return out
```

```python
from contextlib import ExitStack

import concourse.bass as bass
from concourse import mybir

F32 = mybir.dt.float32
F32R = mybir.dt.float32r
ALU = mybir.AluOpType
ACT = mybir.ActivationFunctionType
AX = mybir.AxisListType

B, T, E = 8, 256, 512
H, HS = 32, 16
KVH = 8
P = 128
C = E // P
TT = T // P
MAA, DEC = 32, 64
EPS0, EPS1 = 1e-5, 1e-6
QSCALE = HS ** -0.5
STREAMS = [2, 0, 1, 3, 4]
VS, KS, WS, RS, GS = range(5)
UNITS = 2 * C
DH = HS // 2
AUNITS = TT * KVH
GRP = H // KVH

VECS = ["ln1_w", "ln1_b", "ln2_w", "ln2_b", "maa_x", "stack0", "stack1", "stack2", "stack3", "stack4",
        "time_decay", "faaaa", "ffn_maa_k", "ffn_maa_r", "bq"]
NVEC = len(VECS) * C + 1
BK_COL = len(VECS) * C

PER = dict(
    ctx_in=16, s0_in=16, x_in=16, k_out=16, k4_in=128, v_out=16, vb0_in=8 * UNITS, vb1_in=8 * UNITS, mask_in=16,
    q_out=32, q4_in=128, y_out=16,
    k_ps=1, v_ps=1, k_hi=1, k_lo=1, v_aug=1,
    var=4, rstd=4, xn=2, xT_ps=2, xnT=2, sx=2, xm=1, m1_ps=1, th=1,
    w2_ps=5, x5m=5, x5=5, proj_ps=5, hid=1, z_ps=1, proj=5, gate=1,
    ruk=1, bonus_ps=1, bonus=1,
    kv=UNITS, y=UNITS, red=UNITS,
    att=1, att_ps=1, cen=1, sq=1, cenr=1, attg=1, aT_ps=2, aT=2, wo_ps=2, x1=1,
    xk=1, xr=1, kk_ps=1, relu=1, kk=1, rr_ps=1, rr=1, fv_ps=1, x2=1,
    x2T_ps=1, x2T=1, q_ps=1, q_hi=1, q_lo=1,
    sc_ps=AUNITS, neg=AUNITS, pr=AUNITS, pt_ps=AUNITS, pt0=AUNITS, pt1=AUNITS, pv=AUNITS,
    ot=AUNITS // 4, ot_ps=AUNITS // 4, at=AUNITS // 4,
    y1=1, y1b=1, yn=1, y_done=1,
)


def build(nc, d):
    ctx = ExitStack()
    with ctx:
        def sb(name, shape, dt=F32, where=ctx):
            return where.enter_context(nc.sbuf_tensor(name, shape, dt))

        big = ["WrT", "WkT", "WvT", "WgT", "WoT", "fWkT", "fWrT", "fWvT", "Wq", "Wo1"]
        W = {n: sb(n, [P, C, E]) for n in big}
        Wk1, Wv1 = sb("Wk1", [P, C, P]), sb("Wv1", [P, C, P])
        mw1 = sb("mw1", [P, C, 5 * MAA])
        mw2 = sb("mw2", [P, 2, E])
        dw1 = sb("dw1", [P, C, DEC])
        dw2 = sb("dw2", [P, E])
        vec = sb("vec", [P, NVEC])
        rows = sb("rows", [P, 5, E])
        bv_r = sb("bv_r", [P, P])
        ident = sb("ident", [P, P])
        pick = sb("pick", [P, P + HS])
        hones = sb("hones", [P, P])
        bq4 = sb("bq4", [P, C])
        half = sb("half", [P, 2 * H])

        x_in = sb("x_in_t", [P, TT, E])
        res = sb("res", [P, TT, E])
        tok = sb("tok", [P, TT, E])
        xnT = sb("xnT_t", [P, C, T + 1])
        sx = sb("sx_t", [P, C, T])
        mask = sx[:, 0:2, :]
        OT = sx[:, 2:4, :].rearrange("p a t -> p (a t)")
        xa, xb = sb("xa", [P, C, T]), sb("xb", [P, C, T])
        kT, vT, rT, wT = (sb(n, [P, C, T]) for n in ("kT", "vT", "rT", "wT"))
        g = sb("g", [P, TT, E])
        th = sb("th_t", [P, 5, T])
        hid = sb("hid_t", [P, T])
        s0 = sb("s0", [P, C, HS])
        prev = sb("prev", [P, C, 1])
        vaug = sb("vaug_t", [P, TT, KVH, 2 * HS])
        K4 = sb("K4", [P, KVH, 2, T], F32R)
        stat = sb("stat", [P, TT, 6])
        mv = sb("mv", [P, TT, 2])
        ve = sb("ve", [P, 2 * H])
        rs = sb("rs", [P, 2 * H])
        mean = sb("mean", [P, 2 * H])
        nmax = sb("nmax", [P, 2, GRP])
        rc = sb("rc", [P, GRP, 4])
        with ExitStack() as first:
            AB = sb("AB", [P, 2, DH, T], F32, first)
            S = sb("S", [P, DH, T], F32, first)
        Q4 = sb("Q4", [P, H // 2, T], F32R)
        SM = sb("SM", [P, 2, GRP, T])
        PT = sb("PT", [P, 2, E])

        ps = ctx.enter_context(nc.psum_tensor("ps", [P, 8, 512], F32))
        tm = {n: ps[:, 2 * i:2 * i + 2, :] for i, n in enumerate("ABCD")}
        fm = {n: a.rearrange("p k (a t) -> p (k a) t", a=2) for n, a in tm.items()}

        xb_tm, rT_tm = (a[:].rearrange("p (i a) t -> p i (a t)", i=TT) for a in (xb, rT))

        kscr = nc.dram_tensor("k_scratch", (2, P, T), F32, kind="Internal").ap()
        vscr = nc.dram_tensor("v_scratch", (E, T), F32, kind="Internal").ap()
        qscr = nc.dram_tensor("q_scratch", (2, E, T), F32, kind="Internal").ap()

        sem = {n: ctx.enter_context(nc.semaphore("s_" + n)) for n in PER}
        s_w1, s_w2, s_const, s_seen, s_bq4, s_cst, s_past = (
            ctx.enter_context(nc.semaphore(n)) for n in ("w_early", "w_late", "consts", "seen", "bq4_done", "pool_const", "past"))
        s_v, s_p, s_a = (ctx.enter_context(nc.semaphore(n)) for n in ("vector_step", "pool_step", "scalar_step"))

        def vcol(name, c):
            i = VECS.index(name) * C + c
            return vec[:, i:i + 1]

        def need(eng, b, name, k):
            v = b * PER[name] + k
            if not isinstance(v, int) or v > 0:
                eng.wait_ge(sem[name], v)
                if eng is nc.sync:
                    eng.sem_inc(s_past, 1)

        class Steps:

            def __init__(self, eng, s):
                self.eng, self.s, self.per, self.n, self.b = eng, s, 0, 0, 0

            def start(self, b):
                self.per = max(self.per, self.n)
                self.n, self.b = 0, b

            def did(self, ins):
                ins.then_inc(self.s, 1)
                self.n += 1

            def wait(self):
                self.eng.wait_ge(self.s, self.b * self.per + self.n)

            def then(self, ins):
                self.did(ins)
                self.wait()

        def batches(eng, body):
            body(0)
            with eng.Fori(1, B) as b:
                body(b)

        block = ctx.enter_context(nc.Block())

        @block.sync
        def _(sp):
            early = [(vec[:], d["vec"]), (mw1[:], d["mw1"]), (Wk1[:], d["Wk1"]), (Wv1[:], d["Wv1"]),
                     (mw2[:], d["mw2"]), (dw1[:], d["dw1"]), (dw2[:], d["dw2"]),
                     (W["WvT"][:], d["WvT"]), (W["WkT"][:], d["WkT"]),
                     (bv_r[:], d["bv"].rearrange("(a n) -> a n", a=1).to_broadcast([P, P]))]
            late = [(W[n][:], d[n]) for n in ("WrT", "WgT", "WoT", "fWkT", "fWrT", "fWvT", "Wq", "Wo1")]
            late += [(rows[:, i, :], d[n].rearrange("(a n) -> a n", a=1).to_broadcast([P, E]))
                     for i, n in enumerate(("gn_w", "gn_b", "bo", "gamma", "beta"))]

            def batch(b):
                first = isinstance(b, int)
                need(sp, b, "q_ps", 0)
                sp.dma_start(xa[:], d["ctxT"][b]).then_inc(sem["ctx_in"], 16)
                need(sp, b, "red", 0)
                sp.dma_start(s0[:], d["s0"][b]).then_inc(sem["s0_in"], 16)
                need(sp, b, "x1", 0)
                sp.dma_start(x_in[:], d["x"][b]).then_inc(sem["x_in"], 16)
                if first:
                    for dst, src in early:
                        sp.dma_start(dst, src).then_inc(s_w1, 16)
                    for dst, src in late:
                        sp.dma_start(dst, src).then_inc(s_w2, 16)
                need(sp, b, "k_hi", 1)
                need(sp, b, "k_lo", 1)
                need(sp, b, "k4_in", 0)
                sp.dma_start(kscr.rearrange("a p t -> p a t"), wT[:, 1:3, :]).then_inc(sem["k_out"], 16)
                need(sp, b, "k_out", 16)
                need(sp, b, "sc_ps", 0)
                if first:
                    sp.wait_ge(s_const, 1)
                for h2 in range(2):
                    for part in range(4):
                        at = h2 * 64 + part * 16
                        sp.dma_start(K4[at:at + 16, :, h2, :].bitcast(F32),
                                     kscr[part % 2].rearrange("(g k) t -> k g t", k=HS)).then_inc(sem["k4_in"], 16)
                need(sp, b, "proj", VS + 1)
                need(sp, b, "vb0_in", 0)
                need(sp, b, "vb1_in", 0)
                sp.dma_start(vscr.rearrange("(c p) t -> p c t", p=P), vT[:]).then_inc(sem["v_out"], 16)
                need(sp, b, "v_out", 16)
                need(sp, b, "pv", 0)
                need(sp, b, "pr", 0)
                for u in range(UNITS):
                    c, dh = divmod(u, 2)
                    if u >= 2:
                        need(sp, b, "red", u - 1)
                    src = vscr[c * P:(c + 1) * P, :].rearrange("(h e d) t -> h e (d t)", e=2, d=DH)[:, dh, :]
                    sp.dma_start(AB[:, u % 2, :, :].rearrange("p d t -> p (d t)"),
                                 src.unsqueeze(1).to_broadcast([P // HS, HS, DH * T])
                                 ).then_inc(sem[f"vb{u % 2}_in"], 16)
                need(sp, b, "xr", 1)
                need(sp, b, "xk", 1)
                sp.dma_start(mask, d["mask"][b]).then_inc(sem["mask_in"], 16)
                need(sp, b, "q_hi", 1)
                need(sp, b, "q4_in", 0)
                sp.dma_start(qscr[0].rearrange("(c p) t -> p c t", p=P), kT[:]).then_inc(sem["q_out"], 16)
                need(sp, b, "q_lo", 1)
                sp.dma_start(qscr[1].rearrange("(c p) t -> p c t", p=P), rT[:]).then_inc(sem["q_out"], 16)
                need(sp, b, "q_out", 32)
                need(sp, b, "red", UNITS)
                for h2 in range(2):
                    for part in range(4):
                        at = h2 * 64 + part * 16
                        src = qscr[part // 2].rearrange("(p h k) t -> h k p t", h=2, k=HS)[h2]
                        sp.dma_start(Q4[at:at + 16, :, :].bitcast(F32), src).then_inc(sem["q4_in"], 16)

            batches(sp, batch)
            sp.wait_ge(sem["q4_in"], B * PER["q4_in"])
            sp.wait_ge(sem["y_out"], B * PER["y_out"])

        @block.gpsimd
        def _(pool):
            gp = nc.gpsimd
            st = Steps(pool, s_p)
            n = [0]

            def const(ins):
                n[0] += 1
                ins.then_inc(s_cst, 1)

            const(gp.memset(ident[:], 0.0))
            const(gp.memset(pick[:], 0.0))
            const(gp.memset(hones[:], 1.0))
            const(gp.memset(half[:], -0.5))
            const(gp.memset(th[:], 0.0))
            const(gp.memset(hid[:], 0.0))
            const(gp.memset(vaug[:], 1.0))
            const(gp.memset(K4[:].bitcast(F32), 0.0))
            pool.wait_ge(s_cst, n[0])
            heads = pick[:, HS - 1:HS - 1 + P].rearrange("p (h j) -> p h j", j=HS)[:, :, 0]
            const(gp.affine_select(out=ident[:], in_=ident[:], compare_op=ALU.not_equal, fill=1.0, base=0,
                                   pattern=[[-1, P]], channel_multiplier=1))
            const(gp.memset(heads, 1.0))
            pool.wait_ge(s_cst, n[0])
            nh = P // HS
            h3 = hones[:].rearrange("p (h j) -> p h j", j=HS)
            const(gp.affine_select(out=heads, in_=heads, compare_op=ALU.is_ge, fill=0.0, base=0,
                                   pattern=[[-HS, nh]], channel_multiplier=1))
            const(gp.affine_select(out=h3, in_=h3, compare_op=ALU.is_ge, fill=0.0, base=0,
                                   pattern=[[-HS, nh], [0, HS]], channel_multiplier=1))
            pool.wait_ge(s_cst, n[0])
            const(gp.affine_select(out=heads, in_=heads, compare_op=ALU.is_ge, fill=0.0, base=HS - 1,
                                   pattern=[[HS, nh]], channel_multiplier=-1))
            const(gp.affine_select(out=h3, in_=h3, compare_op=ALU.is_ge, fill=0.0, base=HS - 1,
                                   pattern=[[HS, nh], [0, HS]], channel_multiplier=-1))
            pool.wait_ge(s_cst, n[0])
            pool.sem_inc(s_const, 1)

            def rsqrt(b, k, w):
                need(pool, b, "var", k)
                gp.tensor_tensor(rs[:, 0:w], ve[:, 0:w], half[:, 0:w], ALU.pow).then_inc(sem["rstd"], 1)

            def row(i):
                return rows[:, i:i + 1, :].to_broadcast([P, TT, E])

            def batch(b):
                st.start(b)
                rsqrt(b, 1, TT)
                for j in range(5):
                    x5 = (xa, xb)[j % 2]
                    need(pool, b, "x5m", j + 1)
                    gp.tensor_tensor(x5[:], x5[:], xnT[:, :, 1:T + 1], ALU.add).then_inc(sem["x5"], 1)
                need(pool, b, "proj", KS + 1)
                for u in range(UNITS):
                    need(pool, b, f"vb{u % 2}_in", 16 * (u // 2 + 1))
                    ab = AB[:, u % 2, :, :]
                    gp.tensor_tensor(ab, ab, kT[:, u // 2:u // 2 + 1, :].to_broadcast([P, DH, T]),
                                     ALU.mult).then_inc(sem["kv"], 1)
                rsqrt(b, 2, 2 * H)
                need(pool, b, "cenr", 1)
                if isinstance(b, int):
                    pool.wait_ge(s_w2, 16 * 13)
                need(pool, b, "gate", 1)
                st.then(gp.tensor_tensor(xb_tm, xb_tm, row(0), ALU.mult))
                st.then(gp.tensor_tensor(xb_tm, xb_tm, row(1), ALU.add))
                gp.tensor_tensor(xb_tm, xb_tm, g[:], ALU.mult).then_inc(sem["attg"], 1)
                rsqrt(b, 3, TT)
                need(pool, b, "relu", 1)
                gp.tensor_tensor(kT[:], kT[:], kT[:], ALU.mult).then_inc(sem["kk"], 1)
                need(pool, b, "y1", 1)
                gp.tensor_tensor(res[:], res[:], row(2), ALU.add).then_inc(sem["y1b"], 1)
                rsqrt(b, 4, TT)
                need(pool, b, "yn", 1)
                st.then(gp.tensor_tensor(tok[:], tok[:], row(3), ALU.mult))
                gp.tensor_tensor(tok[:], tok[:], row(4), ALU.add).then_inc(sem["y_done"], 1)

            batches(pool, batch)

        @block.scalar
        def _(act):
            sc = nc.scalar
            st = Steps(act, s_a)

            def batch(b):
                st.start(b)
                if isinstance(b, int):
                    act.wait_ge(s_w1, 16 * 10)
                    for c in range(C):
                        ins = sc.mul(bq4[:, c:c + 1], vcol("bq", c), QSCALE)
                    ins.then_inc(s_bq4, 1)
                need(act, b, "k_ps", 1)
                st.then(sc.activation(wT[:, 0, :], ps[:, 6, 0:T], ACT.Identity, bias=vec[:, BK_COL:BK_COL + 1]))
                sc.copy(wT[:, 1, :].bitcast(F32R), wT[:, 0, :]).then_inc(sem["k_hi"], 1)

                def shifted(k, w, bias, col):
                    need(act, b, "xT_ps", k)
                    for c in range(C):
                        sc.activation(xnT[:, c, 1:T + 1], fm["A"][:, c, :], ACT.Identity, bias=vcol(bias, c),
                                      scale=vcol(w, c))
                    sc.copy(xnT[:, :, 0:1], col).then_inc(sem["xnT"], 1)

                need(act, b, "ctx_in", 16)
                st.then(sc.copy(prev[:], xa[:, :, 0:1]))
                shifted(1, "ln1_w", "ln1_b", xa[:, :, 1:2])
                need(act, b, "m1_ps", 1)
                if isinstance(b, int):
                    act.wait_ge(s_const, 1)
                for j in range(4):
                    sc.activation(th[32 * j:32 * j + 32, j, :], ps[32 * j:32 * j + 32, 2, 0:T], ACT.Tanh)
                sc.activation(th[0:32, 4, :], ps[0:32, 3, 0:T], ACT.Tanh).then_inc(sem["th"], 1)
                need(act, b, "proj_ps", VS + 1)
                sc.copy(vT[:], fm["A"]).then_inc(sem["proj"], 1)
                need(act, b, "proj_ps", KS + 1)
                sc.copy(kT[:], fm["B"]).then_inc(sem["proj"], 1)
                need(act, b, "proj_ps", WS + 1)
                sc.activation(hid[0:DEC, :], ps[0:DEC, 0, 0:T], ACT.Tanh).then_inc(sem["hid"], 1)
                need(act, b, "z_ps", 1)
                need(act, b, "k_out", 16)
                for c in range(C):
                    ins = sc.activation(wT[:, c, :], fm["A"][:, c, :], ACT.Exp, bias=vcol("time_decay", c))
                st.then(ins)
                sc.activation(wT[:], wT[:], ACT.Exp, scale=-1.0).then_inc(sem["proj"], 1)
                need(act, b, "proj_ps", RS + 1)
                sc.copy(rT[:], fm["B"]).then_inc(sem["proj"], 1)
                need(act, b, "proj_ps", GS + 1)
                sc.activation(g[:], tm["A"], ACT.Tanh, scale=0.5).then_inc(sem["proj"], 1)
                need(act, b, "cen", 1)
                sc.activation(tok[:], xb_tm, ACT.Square).then_inc(sem["sq"], 1)
                need(act, b, "aT_ps", 1)
                sc.copy(xa[:], fm["A"]).then_inc(sem["aT"], 1)
                shifted(2, "ln2_w", "ln2_b", prev[:])
                need(act, b, "kk_ps", 1)
                sc.activation(kT[:], fm["C"], ACT.Relu).then_inc(sem["relu"], 1)
                need(act, b, "rr_ps", 1)
                sc.activation(rT_tm, tm["D"], ACT.Tanh, scale=0.5).then_inc(sem["rr"], 1)
                need(act, b, "x2T_ps", 1)
                sc.copy(xa[:], fm["B"]).then_inc(sem["x2T"], 1)
                need(act, b, "q_ps", 1)
                if isinstance(b, int):
                    act.wait_ge(s_bq4, 1)
                for c in range(C):
                    ins = sc.activation(xb[:, c, :], fm["C"][:, c, :], ACT.Identity, bias=bq4[:, c:c + 1],
                                        scale=QSCALE)
                st.then(ins)
                sc.copy(kT[:].bitcast(F32R), xb[:]).then_inc(sem["q_hi"], 1)
                for i in range(AUNITS + 2):
                    if i < AUNITS:
                        need(act, b, "neg", i + 1)
                        for h in range(GRP):
                            ins = sc.activation(SM[:, i % 2, h, :], SM[:, i % 2, h, :], ACT.Exp, scale=-1.0,
                                                bias=nmax[:, i % 2, h:h + 1])
                        ins.then_inc(sem["pr"], 1)
                    if 1 <= i <= AUNITS:
                        need(act, b, "pt_ps", i)
                        need(act, b, "pv", i - 1)
                        sc.copy(PT[:, 0, :], ps[:, 4, :]).then_inc(sem["pt0"], 1)
                    if i >= 2 and (i - 2) % 4 == 3:
                        need(act, b, "pv", i - 1)
                        sc.copy(OT, ps[:, 6, :]).then_inc(sem["ot"], 1)
                need(act, b, "aT_ps", 2)
                sc.copy(xb[:], fm["A"]).then_inc(sem["aT"], 1)
                need(act, b, "y_done", 1)
                act.dma_start(d["out"][b], tok[:]).then_inc(sem["y_out"], 16)

            batches(act, batch)

        @block.vector
        def _(dve):
            ve_ = nc.vector
            st = Steps(dve, s_v)

            def batch(b):
                st.start(b)

                def norm(k, src, eps, out, signal):
                    for i in range(TT):
                        st.did(ve_.bn_stats(stat[:, i, :], src[:, i, :]))
                    st.wait()
                    dve.sem_inc(s_seen, 1)
                    for i in range(TT):
                        st.did(ve_.bn_aggr(mv[:, i, :], stat[:, i, :]))
                    st.wait()
                    ve_.tensor_scalar(ve[:, 0:TT], mv[:, :, 1], eps, None, ALU.add).then_inc(sem["var"], 1)
                    need(dve, b, "rstd", k)
                    for i in range(TT):
                        ins = ve_.tensor_scalar(out[:, i, :], src[:, i, :], mv[:, i, 0:1], rs[:, i:i + 1],
                                                ALU.subtract, ALU.mult)
                    ins.then_inc(sem[signal], 1)

                def shift(k):
                    need(dve, b, "xnT", k)
                    st.then(ve_.tensor_tensor(sx[:], xnT[:, :, 0:T], xnT[:, :, 1:T + 1], ALU.subtract))

                def mixed(out, name, signal):
                    for c in range(C):
                        ins = ve_.scalar_tensor_tensor(out=out[:, c, :], in0=sx[:, c, :], scalar=vcol(name, c),
                                                       in1=xnT[:, c, 1:T + 1], op0=ALU.mult, op1=ALU.add)
                    ins.then_inc(sem[signal], 1)

                need(dve, b, "v_ps", 1)
                if isinstance(b, int):
                    dve.wait_ge(s_w1, 16 * 10)
                    dve.wait_ge(s_const, 1)
                ve_.tensor_tensor(vaug[:, :, :, 0:HS],
                                  ps[:, 4, 0:TT * P].rearrange("p (i g d) -> p i g d", i=TT, d=HS),
                                  bv_r[:].rearrange("p (i g d) -> p i g d", i=1, d=HS).to_broadcast([P, TT, KVH, HS]),
                                  ALU.add).then_inc(sem["v_aug"], 1)
                need(dve, b, "k_hi", 1)
                ve_.tensor_tensor(wT[:, 2, :].bitcast(F32R), wT[:, 0, :], wT[:, 1, :],
                                  ALU.subtract).then_inc(sem["k_lo"], 1)
                need(dve, b, "x_in", 16)
                need(dve, b, "y_out", 0)
                norm(1, x_in, EPS0, tok, "xn")
                shift(1)
                mixed(xb, "maa_x", "xm")
                for j, s in enumerate(STREAMS):
                    need(dve, b, "w2_ps", j + 1)
                    need(dve, b, "proj_ps", j - 1)
                    for c in range(C):
                        ins = ve_.scalar_tensor_tensor(out=(xa, xb)[j % 2][:, c, :], in0=fm["CD"[j % 2]][:, c, :],
                                                       scalar=vcol(f"stack{s}", c), in1=sx[:, c, :],
                                                       op0=ALU.add, op1=ALU.mult)
                    ins.then_inc(sem["x5m"], 1)
                need(dve, b, "proj", RS + 1)
                ruk = tok[:].rearrange("p i (a t) -> p (i a) t", t=T)
                for c in range(C):
                    ins = ve_.scalar_tensor_tensor(out=ruk[:, c, :], in0=rT[:, c, :], scalar=vcol("faaaa", c),
                                                   in1=kT[:, c, :], op0=ALU.mult, op1=ALU.mult)
                ins.then_inc(sem["ruk"], 1)
                need(dve, b, "proj", GS + 1)
                st.then(ve_.tensor_scalar(g[:], g[:], 0.5, 0.5, ALU.mult, ALU.add))
                ve_.tensor_tensor(g[:], tm["A"], g[:], ALU.mult).then_inc(sem["gate"], 1)
                need(dve, b, "bonus_ps", 1)
                ve_.tensor_tensor(ruk, fm["B"], vT[:], ALU.mult).then_inc(sem["bonus"], 1)
                need(dve, b, "s0_in", 16)
                for u in range(UNITS):
                    c, dh = divmod(u, 2)
                    ab = AB[:, u % 2, :, :]
                    begin = s0[:, c, dh * DH:dh * DH + DH]
                    st.did(ve_.tensor_copy(S[:, :, 0], begin))
                    need(dve, b, "kv", u + 1)
                    for k in range(DH):
                        st.did(ve_.tensor_tensor_scan(S[:, k, 1:T], wT[:, c, 0:T - 1], ab[:, k, 0:T - 1],
                                                      begin[:, k:k + 1], ALU.mult, ALU.add))
                    st.wait()
                    ve_.tensor_tensor(ab, S[:], rT[:, c:c + 1, :].to_broadcast([P, DH, T]),
                                      ALU.mult).then_inc(sem["y"], 1)
                    need(dve, b, "y", u + 1)
                need(dve, b, "red", UNITS)
                ve_.tensor_tensor(xa[:], fm["C"], ruk, ALU.add).then_inc(sem["att"], 1)
                need(dve, b, "att_ps", 1)
                att = tm["D"].rearrange("p i (h d) -> p (i h) d", d=HS)
                cen = xb_tm.rearrange("p i (h d) -> p (i h) d", d=HS)
                st.then(ve_.tensor_reduce(mean[:], att, AX.X, ALU.add))
                st.then(ve_.tensor_scalar(mean[:], mean[:], 1.0 / HS, None, ALU.mult))
                ve_.tensor_tensor(cen, att, mean[:].unsqueeze(2).to_broadcast([P, TT * H, HS]),
                                  ALU.subtract).then_inc(sem["cen"], 1)
                need(dve, b, "sq", 1)
                st.then(ve_.tensor_reduce(ve[:], tok[:].rearrange("p i (h d) -> p (i h) d", d=HS), AX.X, ALU.add))
                ve_.tensor_scalar(ve[:], ve[:], 1.0 / HS, EPS0, ALU.mult, ALU.add).then_inc(sem["var"], 1)
                need(dve, b, "rstd", 2)
                ve_.tensor_tensor(cen, cen, rs[:].unsqueeze(2).to_broadcast([P, TT * H, HS]),
                                  ALU.mult).then_inc(sem["cenr"], 1)
                need(dve, b, "wo_ps", 1)
                ve_.tensor_tensor(res[:], x_in[:], tm["B"], ALU.add).then_inc(sem["x1"], 1)
                need(dve, b, "x1", 1)
                norm(3, res, EPS0, tok, "xn")
                shift(2)
                mixed(xa, "ffn_maa_k", "xk")
                mixed(xb, "ffn_maa_r", "xr")
                need(dve, b, "rr", 1)
                st.then(ve_.tensor_scalar(rT_tm, rT_tm, 0.5, 0.5, ALU.mult, ALU.add))
                need(dve, b, "fv_ps", 1)
                st.then(ve_.tensor_tensor(rT_tm, tm["A"], rT_tm, ALU.mult))
                ve_.tensor_tensor(res[:], res[:], rT_tm, ALU.add).then_inc(sem["x2"], 1)
                need(dve, b, "q_hi", 1)
                ve_.tensor_tensor(rT[:].bitcast(F32R), xb[:], kT[:], ALU.subtract).then_inc(sem["q_lo"], 1)
                need(dve, b, "mask_in", 16)
                for i in range(AUNITS + 3):
                    if i < AUNITS:
                        need(dve, b, "sc_ps", i + 1)
                        need(dve, b, "pt_ps", i - 1)
                        dve.sem_inc(s_seen, 1)
                        for h in range(GRP):
                            sps = tm["AB"[i % 2]][:, h // 2, (h % 2) * T:(h % 2) * T + T]
                            ins = ve_.tensor_tensor_reduce(
                                out=SM[:, i % 2, h, :], in0=sps, in1=mask[:, i // KVH, :], scale=-1.0,
                                scalar=3.0e38, op0=ALU.add, op1=ALU.min, accum_out=nmax[:, i % 2, h:h + 1])
                        ins.then_inc(sem["neg"], 1)
                    if 1 <= i <= AUNITS:
                        need(dve, b, "pt_ps", i)
                        need(dve, b, "pv", i - 1)
                        ve_.tensor_copy(PT[:, 1, :], ps[:, 5, :]).then_inc(sem["pt1"], 1)
                    if i >= 3 and (i - 3) % 4 == 3:
                        n = (i - 3) // 4
                        qt, gs = divmod(n, 2)
                        need(dve, b, "ot_ps", n + 1)
                        o = ps[:, 7, :].rearrange("p (h g e) -> p h g e", h=GRP, g=4)
                        st.then(ve_.reciprocal(rc[:], o[:, :, :, HS]))
                        ve_.tensor_tensor(g[:, qt, gs * 256:gs * 256 + 256].rearrange("p (g h d) -> p h g d", g=4, h=GRP),
                                          o[:, :, :, 0:HS], rc[:].unsqueeze(3).to_broadcast([P, GRP, 4, HS]),
                                          ALU.mult).then_inc(sem["at"], 1)
                need(dve, b, "wo_ps", 2)
                ve_.tensor_tensor(res[:], res[:], tm["B"], ALU.add).then_inc(sem["y1"], 1)
                need(dve, b, "y1b", 1)
                norm(4, res, EPS1, tok, "yn")

            batches(dve, batch)

        @block.tensor
        def _(pe):
            mm = nc.tensor.matmul

            def batch(b):
                def features(out, w, x):
                    for c in range(C):
                        for k in range(C):
                            ins = mm(out[:, c, :], w[:, k, c * P:(c + 1) * P], x[:, k, :], start=(k == 0), stop=(k == C - 1))
                    return ins

                def tokens(out, x, w):
                    for i in range(TT):
                        for k in range(C):
                            ins = mm(out[:, i, :], x[:, k, i * P:(i + 1) * P], w[:, k, :], start=(k == 0), stop=(k == C - 1))
                    return ins

                def to_features(out, x):
                    for i in range(TT):
                        for c in range(C):
                            ins = nc.tensor.transpose(out[:, c, i * P:(i + 1) * P], x[:, i, c * P:(c + 1) * P], ident[:])
                    return ins

                def to_tokens(out, x):
                    for i in range(TT):
                        for c in range(C):
                            ins = nc.tensor.transpose(out[:, i, c * P:(c + 1) * P], x[:, c, i * P:(i + 1) * P], ident[:])
                    return ins

                if isinstance(b, int):
                    pe.wait_ge(s_w1, 16 * 10)
                    pe.wait_ge(s_const, 1)
                need(pe, b, "ctx_in", 16)
                need(pe, b, "ot", 0)
                need(pe, b, "pt0", 0)
                for k in range(C):
                    ins = mm(ps[:, 6, 0:T], Wk1[:, k, :], xa[:, k, :], start=(k == 0), stop=(k == C - 1))
                ins.then_inc(sem["k_ps"], 1)
                for i in range(TT):
                    for k in range(C):
                        ins = mm(ps[:, 4, i * P:(i + 1) * P], xa[:, k, i * P:(i + 1) * P], Wv1[:, k, :],
                                 start=(k == 0), stop=(k == C - 1))
                ins.then_inc(sem["v_ps"], 1)
                need(pe, b, "xn", 1)
                need(pe, b, "aT", 0)
                to_features(fm["A"], tok).then_inc(sem["xT_ps"], 1)
                need(pe, b, "xm", 1)
                need(pe, b, "y1", 0)
                for k in range(C):
                    mm(ps[:, 2, 0:T], mw1[:, k, 0:P], xb[:, k, :], start=(k == 0), stop=(k == C - 1))
                for k in range(C):
                    ins = mm(ps[0:MAA, 3, 0:T], mw1[:, k, P:P + MAA], xb[:, k, :], start=(k == 0), stop=(k == C - 1))
                ins.then_inc(sem["m1_ps"], 1)

                def spread(j):
                    s = STREAMS[j]
                    if j >= 2:
                        need(pe, b, "x5m", j - 1)
                    for c in range(C):
                        ins = mm(fm["CD"[j % 2]][:, c, :], mw2[:, s // 4, c * P:(c + 1) * P], th[:, s, :], start=True, stop=True)
                    ins.then_inc(sem["w2_ps"], 1)

                need(pe, b, "th", 1)
                need(pe, b, "v_aug", 1)
                spread(0)
                need(pe, b, "k_hi", 1)
                for j in range(5):
                    if j < 4:
                        spread(j + 1)
                    if j == RS and isinstance(b, int):
                        pe.wait_ge(s_w2, 16 * 13)
                    need(pe, b, "x5", j + 1)
                    if j >= 2:
                        need(pe, b, "proj", j - 1)
                    if j == GS:
                        need(pe, b, "proj", WS + 1)
                    x5, out = (xa, xb)[j % 2], "AB"[j % 2]
                    if j == WS:
                        for k in range(C):
                            ins = mm(ps[0:DEC, 0, 0:T], dw1[:, k, :], x5[:, k, :], start=(k == 0), stop=(k == C - 1))
                        ins.then_inc(sem["proj_ps"], 1)
                        need(pe, b, "hid", 1)
                        for c in range(C):
                            ins = mm(fm["A"][:, c, :], dw2[:, c * P:(c + 1) * P], hid[:], start=True, stop=True)
                        ins.then_inc(sem["z_ps"], 1)
                    elif j == GS:
                        tokens(tm[out], x5, W["WgT"]).then_inc(sem["proj_ps"], 1)
                    else:
                        features(fm[out], W[{VS: "WvT", KS: "WkT", RS: "WrT"}[j]], x5).then_inc(sem["proj_ps"], 1)
                need(pe, b, "ruk", 1)
                for c in range(C):
                    ins = mm(fm["B"][:, c, :], hones[:], tok[:].rearrange("p i (a t) -> p (i a) t", t=T)[:, c, :],
                             start=True, stop=True)
                ins.then_inc(sem["bonus_ps"], 1)
                for u in range(UNITS):
                    c, dh = divmod(u, 2)
                    need(pe, b, "y", u + 1)
                    for k in range(DH):
                        dd = dh * DH + k
                        ins = mm(fm["C"][:, c, :], pick[:, HS - 1 - dd:HS - 1 - dd + P], AB[:, u % 2, k, :],
                                 start=(dd == 0), stop=(dd == HS - 1))
                    ins.then_inc(sem["red"], 1)
                need(pe, b, "att", 1)
                to_tokens(tm["D"], xa).then_inc(sem["att_ps"], 1)
                need(pe, b, "attg", 1)
                to_features(fm["A"], xb_tm).then_inc(sem["aT_ps"], 1)
                need(pe, b, "aT", 1)
                tokens(tm["B"], xa, W["WoT"]).then_inc(sem["wo_ps"], 1)
                need(pe, b, "xn", 2)
                to_features(fm["A"], tok).then_inc(sem["xT_ps"], 1)
                need(pe, b, "xk", 1)
                features(fm["C"], W["fWkT"], xa).then_inc(sem["kk_ps"], 1)
                need(pe, b, "xr", 1)
                tokens(tm["D"], xb, W["fWrT"]).then_inc(sem["rr_ps"], 1)
                need(pe, b, "kk", 1)
                tokens(tm["A"], kT, W["fWvT"]).then_inc(sem["fv_ps"], 1)
                need(pe, b, "x2", 1)
                to_features(fm["B"], res).then_inc(sem["x2T_ps"], 1)
                need(pe, b, "x2T", 1)
                features(fm["C"], W["Wq"], xa).then_inc(sem["q_ps"], 1)
                need(pe, b, "k4_in", 128)
                need(pe, b, "q4_in", 128)
                for i in range(AUNITS + 3):
                    if i < AUNITS:
                        qt, kv = divmod(i, KVH)
                        if i >= 2:
                            need(pe, b, "neg", i - 1)
                        for h in range(2):
                            ins = mm(tm["AB"[i % 2]][:, h, :], Q4[:, 2 * kv + h, qt * P:(qt + 1) * P],
                                     K4[:, kv, :, :].rearrange("p a t -> p (a t)"), start=True, stop=True)
                        ins.then_inc(sem["sc_ps"], 1)
                    if 1 <= i <= AUNITS:
                        need(pe, b, "pr", i)
                        if i >= 2:
                            need(pe, b, "pt0", i - 1)
                            need(pe, b, "pt1", i - 1)
                        elif i == 1:
                            need(pe, b, "q_hi", 1)
                        for t in range(2):
                            for h in range(GRP):
                                ins = nc.tensor.transpose(ps[:, 4 + t, h * P:(h + 1) * P],
                                                          SM[:, (i - 1) % 2, h, t * P:(t + 1) * P], ident[:])
                        ins.then_inc(sem["pt_ps"], 1)
                    if i >= 3 and (i - 3) % 4 == 3:
                        n = (i - 3) // 4
                        need(pe, b, "ot", n + 1)
                        if n >= 1:
                            need(pe, b, "at", n)
                        for h in range(GRP):
                            ins = nc.tensor.transpose(ps[:, 7, h * P:(h + 1) * P], OT[:, h * P:(h + 1) * P], ident[:])
                        ins.then_inc(sem["ot_ps"], 1)
                    if 2 <= i < AUNITS + 2:
                        kv = (i - 2) % KVH
                        need(pe, b, "pt0", i - 1)
                        need(pe, b, "pt1", i - 1)
                        at = 32 * (kv % 4)
                        for t in range(2):
                            ins = mm(ps[at:at + 32, 6, :], vaug[:, t, kv, :], PT[:, t, :], start=(t == 0), stop=(t == 1))
                        ins.then_inc(sem["pv"], 1)
                need(pe, b, "at", 4)
                to_features(fm["A"], g).then_inc(sem["aT_ps"], 1)
                need(pe, b, "aT", 2)
                tokens(tm["B"], xb, W["Wo1"]).then_inc(sem["wo_ps"], 1)

            batches(pe, batch)


def kernel(**inputs):
    import numpy as np
    import concourse.bacc as bacc
    from concourse.bass_utils import run_bass_kernel_spmd as run

    a = {n: np.asarray(v) for n, v in inputs.items()}
    L0, L1 = "L0_xattn_", "L1_xattn_"

    def chunks(w):
        return np.ascontiguousarray(w.reshape(C, P, -1).transpose(1, 0, 2))

    arrays = {
        "x": np.ascontiguousarray(a["x"].reshape(B, TT, P, E).transpose(0, 2, 1, 3)),
        "ctxT": np.ascontiguousarray(a["ctx_2048"].reshape(B, T, C, P).transpose(0, 3, 2, 1)),
        "s0": np.ascontiguousarray(a["ctx_2048"][:, 2:2 + HS].reshape(B, C, P, HS).transpose(0, 2, 1, 3)),
        "mask": np.ascontiguousarray(a["mask_Bx1xSxS2_ff0"].reshape(B, TT, P, T).transpose(0, 2, 1, 3)),
        "mw1": chunks(a[L0 + "maa_w1"]),
        "dw1": chunks(a[L0 + "decay_w1"]),
        "dw2": np.concatenate([a[L0 + "decay_w2"], np.zeros((P - DEC, E), np.float32)]),
        "bv": a[L1 + "bv"],
        "gn_w": a[L0 + "gn_w"], "gn_b": a[L0 + "gn_b"], "bo": a[L1 + "bo"], "gamma": a[L1 + "gamma"], "beta": a[L1 + "beta"],
    }
    w2 = np.zeros((P, 2, E), np.float32)
    w2[:, 0] = a[L0 + "maa_w2"][0:4].reshape(P, E)
    w2[0:MAA, 1] = a[L0 + "maa_w2"][4]
    arrays["mw2"] = w2
    for n, k in (("WrT", "Wr"), ("WkT", "Wk"), ("WvT", "Wv"), ("WgT", "Wg"), ("WoT", "Wo"),
                 ("fWkT", "ffn_Wk"), ("fWrT", "ffn_Wr"), ("fWvT", "ffn_Wv")):
        arrays[n] = chunks(a[L0 + k].T)
    for n, k in (("Wq", "Wq"), ("Wk1", "Wk"), ("Wv1", "Wv"), ("Wo1", "Wo")):
        arrays[n] = chunks(a[L1 + k])
    flat = {"bq": a[L1 + "bq"], "faaaa": a[L0 + "faaaa"].reshape(E)}
    for s in range(5):
        flat[f"stack{s}"] = a[L0 + "maa_stack"][s]
    cols = [flat[n] if n in flat else a[L0 + n] for n in VECS]
    arrays["vec"] = np.ascontiguousarray(
        np.concatenate([v.reshape(C, P) for v in cols] + [a[L1 + "bk"].reshape(1, P)]).T)

    nc = bacc.Bacc("TRN2", target_bir_lowering=False, num_devices=1)
    d = {n: nc.dram_tensor("in_" + n, v.shape, F32, kind="ExternalInput").ap() for n, v in arrays.items()}
    d["out"] = nc.dram_tensor("out_y", (B, P, TT, E), F32, kind="ExternalOutput").ap()
    build(nc, d)
    r = run(nc, [{"in_" + n: v for n, v in arrays.items()}], core_ids=[0])
    y = np.asarray(r.results[0]["out_y"])
    return np.ascontiguousarray(y.reshape(B, P, TT, E).transpose(0, 2, 1, 3).reshape(B, T, E))
```

```python
from contextlib import ExitStack

import concourse.bass as bass
from concourse import mybir

F32 = mybir.dt.float32
F32R = mybir.dt.float32r
ALU = mybir.AluOpType
ACT = mybir.ActivationFunctionType
AX = mybir.AxisListType

B, T, E = 8, 256, 512
H, HS = 32, 16
KVH = 8
P = 128
C = E // P
TT = T // P
MAA, DEC = 32, 64
EPS0, EPS1 = 1e-5, 1e-6
N_EARLY, N_LATE = 7, 14
QSCALE = HS ** -0.5
STREAMS = [2, 0, 1, 3, 4]
VS, KS, WS, RS, GS = range(5)
DH = 4
NQ = HS // DH
UNITS = NQ * C
NAB = 3
AUNITS = TT * KVH
GRP = H // KVH
SETS = AUNITS // 4
STEPS = AUNITS + 4

VECS = ["gn_w", "gn_b", "ln1_w", "ln1_b", "ln2_w", "ln2_b", "maa_x", "stack0", "stack1", "stack2", "stack3", "stack4",
        "time_decay", "faaaa", "ffn_maa_k", "ffn_maa_r", "bq"]
NVEC = len(VECS) * C + 1
BK_COL = len(VECS) * C

PER = dict(
    s0_in=16, prev_in=16, x_in=16, ctx_in=16, k_out=16, k4_in=128, v_out=16,
    vb0_in=96, vb1_in=80, vb2_in=80, mask_in=16, q_out=32, q4_in=128, y_out=16,
    k_ps=1, v_ps=1, k_hi=1, k_lo=1, v_aug=1,
    var=3, rstd=3, xn=2, xT_ps=2, xnT=2, xm=1, m1_ps=1, th=1,
    w2_ps=5, x5m=5, x5=5, proj_ps=5, hid=1, z_ps=1, proj=5, gate=1,
    ruk=1, bonus_ps=1, bonus=1, kv=UNITS, y=UNITS, red=UNITS, att=C,
    att_ps=1, cen=1, sq=1, cenr=1, aT_ps=1, aT=1, attg=1, wo_ps=1, x1=1,
    xk=1, xr=1, kk_ps=1, relu=1, kk=1, rr_ps=1, rr=1, fv_ps=1, x2=1,
    x2T_ps=1, x2T=1, q_ps=1, q_hi=1, q_lo=1,
    sc_ps=AUNITS, neg=AUNITS, pr=AUNITS, pt_ps=AUNITS, pt=AUNITS, pv=AUNITS,
    ot=SETS, ot_ps=SETS, ot2=SETS, at=SETS,
    oT_ps=1, oT=1, wo1_ps=1, y1=1, y1b=1, var3=1, rstd3=1, yn=1, y_done=1,
)


def build(nc, d):
    ctx = ExitStack()
    with ctx:
        def sb(name, shape, dt=F32, where=ctx):
            return where.enter_context(nc.sbuf_tensor(name, shape, dt))

        big = ["WrT", "WkT", "WvT", "WgT", "WoT", "fWkT", "fWrT", "fWvT", "Wq", "Wo1"]
        W = {n: sb(n, [P, C, E]) for n in big}
        Wk1, Wv1 = sb("Wk1", [P, C, P]), sb("Wv1", [P, C, P])
        mw1 = sb("mw1", [P, C, 5 * MAA])
        mw2 = sb("mw2", [P, 2, E])
        dw1 = sb("dw1", [P, C, DEC])
        dw2 = sb("dw2", [P, E])
        vec = sb("vec", [P, NVEC])
        rows = sb("rows", [P, 3, E])
        bv_r = sb("bv_r", [P, P])
        ident = sb("ident", [P, P])
        pick = sb("pick", [P, P + HS])
        hones = sb("hones", [P, P])
        bq4 = sb("bq4", [P, C])
        half = sb("half", [P, 2 * H])

        x_in = sb("x_in_t", [P, TT, E])
        res = sb("res", [P, TT, E])
        tok = sb("tok", [P, TT, E])
        xnT = sb("xnT_t", [P, C, T + 1])
        sx = sb("sx_t", [P, C, T])
        mask = sx[:, 0:2, :]
        OT = sx[:, 2:4, :].rearrange("p a t -> p (a t)")
        xab = sb("xab", [P, 2, C, T])
        xa, xb, SM = xab[:, 0, :, :], xab[:, 1, :, :], xab
        kT, vT, rT, wT = (sb(n, [P, C, T]) for n in ("kT", "vT", "rT", "wT"))
        g = sb("g", [P, C, T])
        at = sb("at_t", [P, TT, E])
        th = sb("th_t", [P, 5, T])
        hid = sb("hid_t", [P, T])
        s0 = sb("s0", [P, C, HS])
        prev = sb("prev", [P, C, 2])
        vaug = sb("vaug_t", [P, TT, KVH, 2 * HS])
        K4 = sb("K4", [P, KVH, 2, T], F32R)
        stat = sb("stat", [P, TT, 6])
        mv = sb("mv", [P, TT, 2])
        ve = sb("ve", [P, 2 * H])
        rs = sb("rs", [P, 2 * H])
        mean = sb("mean", [P, 2 * H])
        nmax = sb("nmax", [P, 2, GRP])
        rc = sb("rc", [P, GRP, 4])
        AB = sb("AB", [P, NAB, DH, T])
        S = sb("S", [P, DH, T])
        Q4 = sb("Q4", [P, H // 2, T], F32R)
        PT = sb("PT", [P, 2, E])

        ps = ctx.enter_context(nc.psum_tensor("ps", [P, 8, 512], F32))
        tm = {n: ps[:, 2 * i:2 * i + 2, :] for i, n in enumerate("ABCD")}
        fm = {n: a.rearrange("p k (a t) -> p (k a) t", a=2) for n, a in tm.items()}

        kT_tm, rT_tm = (a[:].rearrange("p (i a) t -> p i (a t)", i=TT) for a in (kT, rT))
        tok_fm = tok[:].rearrange("p i (a t) -> p (i a) t", t=T)

        kscr = nc.dram_tensor("k_scratch", (2, P, T), F32, kind="Internal").ap()
        vscr = nc.dram_tensor("v_scratch", (E, T), F32, kind="Internal").ap()
        qscr = nc.dram_tensor("q_scratch", (2, E, T), F32, kind="Internal").ap()

        sem = {n: ctx.enter_context(nc.semaphore("s_" + n)) for n in PER}
        s_w1, s_w2, s_const, s_seen, s_bq4, s_cst, s_past = (
            ctx.enter_context(nc.semaphore(n)) for n in ("w_early", "w_late", "consts", "seen", "bq4_done", "pool_const", "past"))
        s_v, s_p, s_a = (ctx.enter_context(nc.semaphore(n)) for n in ("vector_step", "pool_step", "scalar_step"))

        def vcol(name, c):
            i = VECS.index(name) * C + c
            return vec[:, i:i + 1]

        def need(eng, b, name, k):
            v = b * PER[name] + k
            if not isinstance(v, int) or v > 0:
                eng.wait_ge(sem[name], v)
                if eng is nc.sync:
                    eng.sem_inc(s_past, 1)

        class Steps:

            def __init__(self, eng, s):
                self.eng, self.s, self.n = eng, s, 0

            def start(self):
                if self.n:
                    self.eng.sem_inc(s_past, 1)
                    self.eng.sem_clear(self.s)
                self.n = 0

            def did(self, ins):
                ins.then_inc(self.s, 1)
                self.n += 1

            def wait(self):
                self.eng.wait_ge(self.s, self.n)

            def then(self, ins):
                self.did(ins)
                self.wait()

        def iterate(eng, body):
            body(0, None)
            body(1, 0)
            with eng.Fori(2, B) as b:
                body(b, b - 1)
            body(None, B - 1)

        block = ctx.enter_context(nc.Block())

        @block.sync
        def _(sp):
            early = [(vec[:], d["vec"]), (mw1[:], d["mw1"]), (mw2[:], d["mw2"]), (dw1[:], d["dw1"]),
                     (dw2[:], d["dw2"]), (W["WvT"][:], d["WvT"]), (W["WkT"][:], d["WkT"])]
            late = [(W[n][:], d[n]) for n in ("WrT", "WgT", "WoT", "fWkT", "fWrT", "fWvT", "Wq", "Wo1")]
            late += [(Wk1[:], d["Wk1"]), (Wv1[:], d["Wv1"]),
                     (bv_r[:], d["bv"].rearrange("(a n) -> a n", a=1).to_broadcast([P, P]))]
            late += [(rows[:, i, :], d[n].rearrange("(a n) -> a n", a=1).to_broadcast([P, E]))
                     for i, n in enumerate(("bo", "gamma", "beta"))]
            assert len(early) == N_EARLY and len(late) == N_LATE

            def unit_in(b, u):
                c, q = divmod(u, NQ)
                if u >= NAB:
                    need(sp, b, "red", u - NAB + 1)
                src = vscr[c * P:(c + 1) * P, :].rearrange("(h e d) t -> h e (d t)", e=NQ, d=DH)[:, q, :]
                sp.dma_start(AB[:, u % NAB, :, :].rearrange("p d t -> p (d t)"),
                             src.unsqueeze(1).to_broadcast([P // HS, HS, DH * T])
                             ).then_inc(sem[f"vb{u % NAB}_in"], 16)

            def body(b, a):
                if b is not None:
                    need(sp, b, "x1", 0)
                    sp.dma_start(x_in[:], d["x"][b]).then_inc(sem["x_in"], 16)
                    need(sp, b, "xnT", 0)
                    sp.dma_start(prev[:], d["prev"][b]).then_inc(sem["prev_in"], 16)
                    need(sp, b, "y", 0)
                    sp.dma_start(s0[:], d["s0"][b]).then_inc(sem["s0_in"], 16)
                    if isinstance(b, int) and b == 0:
                        for dst, src in early:
                            sp.dma_start(dst, src).then_inc(s_w1, 16)
                        for dst, src in late:
                            sp.dma_start(dst, src).then_inc(s_w2, 16)
                if a is not None:
                    need(sp, a, "q_out", 32)
                    need(sp, a, "sc_ps", 0)
                    for h2 in range(2):
                        for part in range(4):
                            at_ = h2 * 64 + part * 16
                            src = qscr[part // 2].rearrange("(p h k) t -> h k p t", h=2, k=HS)[h2]
                            sp.dma_start(Q4[at_:at_ + 16, :, :].bitcast(F32), src).then_inc(sem["q4_in"], 16)
                if b is not None:
                    need(sp, b, "proj", VS + 1)
                    need(sp, b, "red", 0)
                    sp.dma_start(vscr.rearrange("(c p) t -> p c t", p=P), vT[:]).then_inc(sem["v_out"], 16)
                    need(sp, b, "v_out", 16)
                    for u in range(NAB):
                        unit_in(b, u)
                if a is not None:
                    if b is not None:
                        need(sp, b, "x5m", 5)
                    sp.dma_start(mask, d["mask"][a]).then_inc(sem["mask_in"], 16)
                if b is not None:
                    for u in range(NAB, UNITS):
                        unit_in(b, u)
                    need(sp, b, "y", UNITS)
                    sp.dma_start(rT[:], d["ctxT"][b]).then_inc(sem["ctx_in"], 16)
                    need(sp, b, "k_hi", 1)
                    need(sp, b, "k_lo", 1)
                    need(sp, b, "k4_in", 0)
                    sp.dma_start(kscr.rearrange("a p t -> p a t"), wT[:, 1:3, :]).then_inc(sem["k_out"], 16)
                    need(sp, b, "k_out", 16)
                    if a is not None:
                        need(sp, a, "sc_ps", AUNITS)
                    else:
                        sp.wait_ge(s_const, 1)
                    for h2 in range(2):
                        for part in range(4):
                            at_ = h2 * 64 + part * 16
                            sp.dma_start(K4[at_:at_ + 16, :, h2, :].bitcast(F32),
                                         kscr[part % 2].rearrange("(g k) t -> k g t", k=HS)).then_inc(sem["k4_in"], 16)

            iterate(sp, body)
            sp.wait_ge(sem["q4_in"], B * PER["q4_in"])
            sp.wait_ge(sem["y_out"], B * PER["y_out"])

        @block.gpsimd
        def _(pool):
            gp = nc.gpsimd
            st = Steps(pool, s_p)
            n = [0]

            def const(ins):
                n[0] += 1
                ins.then_inc(s_cst, 1)

            const(gp.memset(ident[:], 0.0))
            const(gp.memset(pick[:], 0.0))
            const(gp.memset(hones[:], 1.0))
            const(gp.memset(half[:], -0.5))
            pool.wait_ge(s_cst, n[0])
            heads = pick[:, HS - 1:HS - 1 + P].rearrange("p (h j) -> p h j", j=HS)[:, :, 0]
            const(gp.affine_select(out=ident[:], in_=ident[:], compare_op=ALU.not_equal, fill=1.0, base=0,
                                   pattern=[[-1, P]], channel_multiplier=1))
            const(gp.memset(heads, 1.0))
            pool.wait_ge(s_cst, n[0])
            nh = P // HS
            h3 = hones[:].rearrange("p (h j) -> p h j", j=HS)
            const(gp.affine_select(out=heads, in_=heads, compare_op=ALU.is_ge, fill=0.0, base=0,
                                   pattern=[[-HS, nh]], channel_multiplier=1))
            const(gp.affine_select(out=h3, in_=h3, compare_op=ALU.is_ge, fill=0.0, base=0,
                                   pattern=[[-HS, nh], [0, HS]], channel_multiplier=1))
            pool.wait_ge(s_cst, n[0])
            const(gp.affine_select(out=heads, in_=heads, compare_op=ALU.is_ge, fill=0.0, base=HS - 1,
                                   pattern=[[HS, nh]], channel_multiplier=-1))
            const(gp.affine_select(out=h3, in_=h3, compare_op=ALU.is_ge, fill=0.0, base=HS - 1,
                                   pattern=[[HS, nh], [0, HS]], channel_multiplier=-1))
            const(gp.memset(th[:], 0.0))
            const(gp.memset(hid[:], 0.0))
            const(gp.memset(vaug[:], 1.0))
            const(gp.memset(K4[:].bitcast(F32), 0.0))
            pool.wait_ge(s_cst, n[0])
            pool.sem_inc(s_const, 1)

            def rsqrt(b, k, w, var="var", rstd="rstd"):
                need(pool, b, var, k)
                gp.tensor_tensor(rs[:, 0:w], ve[:, 0:w], half[:, 0:w], ALU.pow).then_inc(sem[rstd], 1)

            def row(i):
                return rows[:, i:i + 1, :].to_broadcast([P, TT, E])

            def body(b, a):
                st.start()
                if b is not None:
                    rsqrt(b, 1, TT)
                    for j in range(5):
                        x5 = (xa, xb)[j % 2]
                        need(pool, b, "x5m", j + 1)
                        gp.tensor_tensor(x5, x5, xnT[:, :, 1:T + 1], ALU.add).then_inc(sem["x5"], 1)
                    need(pool, b, "proj", KS + 1)
                    for u in range(UNITS):
                        need(pool, b, f"vb{u % NAB}_in", 16 * (u // NAB + 1))
                        ab, c = AB[:, u % NAB, :, :], u // NQ
                        gp.tensor_tensor(ab, ab, kT[:, c:c + 1, :].to_broadcast([P, DH, T]),
                                         ALU.mult).then_inc(sem["kv"], 1)
                    rsqrt(b, 2, 2 * H)
                if a is not None:
                    need(pool, a, "y1", 1)
                    gp.tensor_tensor(at[:], at[:], row(0), ALU.add).then_inc(sem["y1b"], 1)
                    rsqrt(a, 1, TT, "var3", "rstd3")
                    need(pool, a, "yn", 1)
                    st.then(gp.tensor_tensor(at[:], at[:], row(1), ALU.mult))
                    gp.tensor_tensor(at[:], at[:], row(2), ALU.add).then_inc(sem["y_done"], 1)
                if b is not None:
                    rsqrt(b, 3, TT)
                    need(pool, b, "relu", 1)
                    gp.tensor_tensor(kT[:], kT[:], kT[:], ALU.mult).then_inc(sem["kk"], 1)

            iterate(pool, body)

        @block.scalar
        def _(act):
            sc = nc.scalar
            st = Steps(act, s_a)

            def shifted(b, k, w, bias, col):
                need(act, b, "xT_ps", k)
                for c in range(C):
                    sc.activation(xnT[:, c, 1:T + 1], fm["A"][:, c, :], ACT.Identity, bias=vcol(bias, c),
                                  scale=vcol(w, c))
                sc.copy(xnT[:, :, 0:1], col).then_inc(sem["xnT"], 1)

            def before(b):
                if isinstance(b, int) and b == 0:
                    act.wait_ge(s_w1, 16 * N_EARLY)
                    for c in range(C):
                        ins = sc.mul(bq4[:, c:c + 1], vcol("bq", c), QSCALE)
                    ins.then_inc(s_bq4, 1)
                need(act, b, "prev_in", 16)
                shifted(b, 1, "ln1_w", "ln1_b", prev[:, :, 1:2])
                need(act, b, "m1_ps", 1)
                if isinstance(b, int) and b == 0:
                    act.wait_ge(s_const, 1)
                for j in range(4):
                    sc.activation(th[32 * j:32 * j + 32, j, :], ps[32 * j:32 * j + 32, 2, 0:T], ACT.Tanh)
                sc.activation(th[0:32, 4, :], ps[0:32, 3, 0:T], ACT.Tanh).then_inc(sem["th"], 1)
                need(act, b, "proj_ps", VS + 1)
                sc.copy(vT[:], fm["A"]).then_inc(sem["proj"], 1)
                need(act, b, "proj_ps", KS + 1)
                need(act, b, "q_out", 0)
                sc.copy(kT[:], fm["B"]).then_inc(sem["proj"], 1)
                need(act, b, "proj_ps", WS + 1)
                sc.activation(hid[0:DEC, :], ps[0:DEC, 0, 0:T], ACT.Tanh).then_inc(sem["hid"], 1)
                need(act, b, "z_ps", 1)
                need(act, b, "k_out", 0)
                for c in range(C):
                    ins = sc.activation(wT[:, c, :], fm["A"][:, c, :], ACT.Exp, bias=vcol("time_decay", c))
                st.then(ins)
                sc.activation(wT[:], wT[:], ACT.Exp, scale=-1.0).then_inc(sem["proj"], 1)
                need(act, b, "proj_ps", RS + 1)
                sc.copy(rT[:], fm["B"]).then_inc(sem["proj"], 1)
                need(act, b, "proj_ps", GS + 1)
                sc.activation(g[:], fm["A"], ACT.Tanh, scale=0.5).then_inc(sem["proj"], 1)

            def attention(a, i):
                if i < AUNITS:
                    need(act, a, "neg", i + 1)
                    for h in range(GRP):
                        ins = sc.activation(SM[:, i % 2, h, :], SM[:, i % 2, h, :], ACT.Exp, scale=-1.0,
                                            bias=nmax[:, i % 2, h:h + 1])
                    ins.then_inc(sem["pr"], 1)
                if 0 <= i - 3 < AUNITS and (i - 3) % 4 == 3:
                    need(act, a, "ot_ps", (i - 3) // 4 + 1)
                    sc.copy(OT, ps[:, 5, :]).then_inc(sem["ot2"], 1)
                if 1 <= i <= AUNITS:
                    need(act, a, "pt_ps", i)
                    need(act, a, "pv", i - 1)
                    sc.copy(PT[:], tm["D"]).then_inc(sem["pt"], 1)
                if 0 <= i - 2 < AUNITS and (i - 2) % 4 == 3:
                    need(act, a, "pv", i - 1)
                    need(act, a, "at", (i - 2) // 4)
                    sc.copy(OT, ps[:, 5, :]).then_inc(sem["ot"], 1)

            def body(b, a):
                st.start()
                if b is not None:
                    before(b)
                if a is not None:
                    for i in range(STEPS):
                        attention(a, i)
                    need(act, a, "oT_ps", 1)
                    sc.copy(xb, fm["A"]).then_inc(sem["oT"], 1)
                if b is not None:
                    need(act, b, "cen", 1)
                    sc.activation(tok[:], kT_tm, ACT.Square).then_inc(sem["sq"], 1)
                    need(act, b, "k_ps", 1)
                    if isinstance(b, int) and b == 0:
                        act.wait_ge(s_w2, 16 * N_LATE)
                    st.then(sc.activation(wT[:, 0, :], ps[:, 4, 0:T], ACT.Identity, bias=vec[:, BK_COL:BK_COL + 1]))
                    sc.copy(wT[:, 1, :].bitcast(F32R), wT[:, 0, :]).then_inc(sem["k_hi"], 1)
                    need(act, b, "aT_ps", 1)
                    for c in range(C):
                        ins = sc.activation(xa[:, c, :], fm["A"][:, c, :], ACT.Identity, bias=vcol("gn_b", c),
                                            scale=vcol("gn_w", c))
                    ins.then_inc(sem["aT"], 1)
                    shifted(b, 2, "ln2_w", "ln2_b", prev[:, :, 0:1])
                    need(act, b, "kk_ps", 1)
                    sc.activation(kT[:], fm["C"], ACT.Relu).then_inc(sem["relu"], 1)
                    need(act, b, "rr_ps", 1)
                    sc.activation(rT_tm, tm["D"], ACT.Tanh, scale=0.5).then_inc(sem["rr"], 1)
                if a is not None:
                    need(act, a, "y_done", 1)
                    act.dma_start(d["out"][a], at[:]).then_inc(sem["y_out"], 16)
                if b is not None:
                    need(act, b, "x2T_ps", 1)
                    sc.copy(xa, fm["B"]).then_inc(sem["x2T"], 1)
                    need(act, b, "q_ps", 1)
                    if isinstance(b, int) and b == 0:
                        act.wait_ge(s_bq4, 1)
                    for c in range(C):
                        ins = sc.activation(xb[:, c, :], fm["C"][:, c, :], ACT.Identity, bias=bq4[:, c:c + 1],
                                            scale=QSCALE)
                    st.then(ins)
                    sc.copy(kT[:].bitcast(F32R), xb).then_inc(sem["q_hi"], 1)
                    need(act, b, "q_hi", 1)
                    need(act, b, "q4_in", 0)
                    act.dma_start(qscr[0].rearrange("(c p) t -> p c t", p=P), kT[:]).then_inc(sem["q_out"], 16)
                    need(act, b, "q_lo", 1)
                    act.dma_start(qscr[1].rearrange("(c p) t -> p c t", p=P), rT[:]).then_inc(sem["q_out"], 16)

            iterate(act, body)

        @block.vector
        def _(dve):
            vv = nc.vector
            st = Steps(dve, s_v)

            def variance(src, eps, signal):
                for i in range(TT):
                    st.did(vv.bn_stats(stat[:, i, :], src[:, i, :]))
                st.wait()
                for i in range(TT):
                    st.did(vv.bn_aggr(mv[:, i, :], stat[:, i, :]))
                st.wait()
                vv.tensor_scalar(ve[:, 0:TT], mv[:, :, 1], eps, None, ALU.add).then_inc(sem[signal], 1)

            def scaled(src, out, signal):
                for i in range(TT):
                    ins = vv.tensor_scalar(out[:, i, :], src[:, i, :], mv[:, i, 0:1], rs[:, i:i + 1],
                                           ALU.subtract, ALU.mult)
                ins.then_inc(sem[signal], 1)

            def shift(b, k):
                need(dve, b, "xnT", k)
                st.then(vv.tensor_tensor(sx[:], xnT[:, :, 0:T], xnT[:, :, 1:T + 1], ALU.subtract))

            def mixed(out, name, signal):
                for c in range(C):
                    ins = vv.scalar_tensor_tensor(out=out[:, c, :], in0=sx[:, c, :], scalar=vcol(name, c),
                                                  in1=xnT[:, c, 1:T + 1], op0=ALU.mult, op1=ALU.add)
                ins.then_inc(sem[signal], 1)

            def before(b):
                need(dve, b, "x_in", 16)
                variance(x_in, EPS0, "var")
                need(dve, b, "rstd", 1)
                scaled(x_in, tok, "xn")
                if isinstance(b, int) and b == 0:
                    dve.wait_ge(s_w1, 16 * N_EARLY)
                shift(b, 1)
                mixed(xb, "maa_x", "xm")
                for j, s in enumerate(STREAMS):
                    need(dve, b, "w2_ps", j + 1)
                    need(dve, b, "proj_ps", j - 1)
                    for c in range(C):
                        ins = vv.scalar_tensor_tensor(out=(xa, xb)[j % 2][:, c, :], in0=fm["CD"[j % 2]][:, c, :],
                                                      scalar=vcol(f"stack{s}", c), in1=sx[:, c, :],
                                                      op0=ALU.add, op1=ALU.mult)
                    ins.then_inc(sem["x5m"], 1)
                need(dve, b, "proj", RS + 1)
                for c in range(C):
                    ins = vv.scalar_tensor_tensor(out=tok_fm[:, c, :], in0=rT[:, c, :], scalar=vcol("faaaa", c),
                                                  in1=kT[:, c, :], op0=ALU.mult, op1=ALU.mult)
                ins.then_inc(sem["ruk"], 1)
                need(dve, b, "proj", GS + 1)
                st.then(vv.tensor_scalar(g[:], g[:], 0.5, 0.5, ALU.mult, ALU.add))
                vv.tensor_tensor(g[:], fm["A"], g[:], ALU.mult).then_inc(sem["gate"], 1)
                need(dve, b, "bonus_ps", 1)
                vv.tensor_tensor(tok_fm, fm["B"], vT[:], ALU.mult).then_inc(sem["bonus"], 1)
                need(dve, b, "s0_in", 16)

            def recurrence(b, u):
                c, q = divmod(u, NQ)
                ab = AB[:, u % NAB, :, :]
                begin = s0[:, c, q * DH:q * DH + DH]
                need(dve, b, "y", u)
                st.did(vv.tensor_copy(S[:, :, 0], begin))
                need(dve, b, "kv", u + 1)
                for k in range(DH):
                    st.did(vv.tensor_tensor_scan(S[:, k, 1:T], wT[:, c, 0:T - 1], ab[:, k, 0:T - 1],
                                                 begin[:, k:k + 1], ALU.mult, ALU.add))
                st.wait()
                vv.tensor_tensor(ab, S[:], rT[:, c:c + 1, :].to_broadcast([P, DH, T]),
                                 ALU.mult).then_inc(sem["y"], 1)

            def collect(b, c):
                need(dve, b, "red", NQ * (c + 1))
                vv.tensor_tensor(tok_fm[:, c, :], ps[:, 4, (c % 2) * T:(c % 2) * T + T], tok_fm[:, c, :],
                                 ALU.add).then_inc(sem["att"], 1)

            def attention(a, i):
                if i < AUNITS:
                    need(dve, a, "sc_ps", i + 1)
                    need(dve, a, "pt_ps", i - 1)
                    dve.sem_inc(s_seen, 1)
                    for h in range(GRP):
                        sps = tm["AB"[i % 2]][:, h // 2, (h % 2) * T:(h % 2) * T + T]
                        ins = vv.tensor_tensor_reduce(
                            out=SM[:, i % 2, h, :], in0=sps, in1=mask[:, i // KVH, :], scale=-1.0,
                            scalar=3.0e38, op0=ALU.add, op1=ALU.min, accum_out=nmax[:, i % 2, h:h + 1])
                    ins.then_inc(sem["neg"], 1)
                if i >= 4 and (i - 4) % 4 == 3:
                    n = (i - 4) // 4
                    qt, gs = divmod(n, 2)
                    need(dve, a, "ot2", n + 1)
                    o = OT.rearrange("p (h g e) -> p h g e", h=GRP, g=4)
                    st.then(vv.reciprocal(rc[:], o[:, :, :, HS]))
                    vv.tensor_tensor(at[:, qt, gs * 256:gs * 256 + 256].rearrange("p (g h d) -> p h g d", g=4, h=GRP),
                                     o[:, :, :, 0:HS], rc[:].unsqueeze(3).to_broadcast([P, GRP, 4, HS]),
                                     ALU.mult).then_inc(sem["at"], 1)

            def body(b, a):
                st.start()
                if b is not None:
                    before(b)
                if a is not None:
                    need(dve, a, "mask_in", 16)
                    need(dve, a, "y_out", 0)
                for i in range(STEPS):
                    if a is not None:
                        attention(a, i)
                    if b is not None:
                        if i < UNITS:
                            recurrence(b, i)
                        if 1 <= i <= UNITS and i % NQ == 0:
                            collect(b, i // NQ - 1)
                if b is not None:
                    need(dve, b, "att_ps", 1)
                    att = tm["D"].rearrange("p i (h d) -> p (i h) d", d=HS)
                    cen = kT_tm.rearrange("p i (h d) -> p (i h) d", d=HS)
                    st.then(vv.tensor_reduce(mean[:], att, AX.X, ALU.add))
                    st.then(vv.tensor_scalar(mean[:], mean[:], 1.0 / HS, None, ALU.mult))
                    vv.tensor_tensor(cen, att, mean[:].unsqueeze(2).to_broadcast([P, TT * H, HS]),
                                     ALU.subtract).then_inc(sem["cen"], 1)
                    need(dve, b, "sq", 1)
                    st.then(vv.tensor_reduce(ve[:], tok[:].rearrange("p i (h d) -> p (i h) d", d=HS), AX.X, ALU.add))
                    vv.tensor_scalar(ve[:], ve[:], 1.0 / HS, EPS0, ALU.mult, ALU.add).then_inc(sem["var"], 1)
                    need(dve, b, "rstd", 2)
                    vv.tensor_tensor(cen, cen, rs[:].unsqueeze(2).to_broadcast([P, TT * H, HS]),
                                     ALU.mult).then_inc(sem["cenr"], 1)
                if a is not None:
                    need(dve, a, "wo1_ps", 1)
                    vv.tensor_tensor(at[:], res[:], tm["B"], ALU.add).then_inc(sem["y1"], 1)
                if b is not None:
                    if isinstance(b, int) and b == 0:
                        dve.wait_ge(s_w2, 16 * N_LATE)
                        dve.wait_ge(s_const, 1)
                    need(dve, b, "v_ps", 1)
                    vv.tensor_tensor(vaug[:, :, :, 0:HS],
                                     ps[:, 5, 0:TT * P].rearrange("p (i g d) -> p i g d", i=TT, d=HS),
                                     bv_r[:].rearrange("p (i g d) -> p i g d", i=1, d=HS).to_broadcast([P, TT, KVH, HS]),
                                     ALU.add).then_inc(sem["v_aug"], 1)
                    need(dve, b, "k_hi", 1)
                    vv.tensor_tensor(wT[:, 2, :].bitcast(F32R), wT[:, 0, :], wT[:, 1, :],
                                     ALU.subtract).then_inc(sem["k_lo"], 1)
                    need(dve, b, "aT", 1)
                    vv.tensor_tensor(xa, xa, g[:], ALU.mult).then_inc(sem["attg"], 1)
                if a is not None:
                    need(dve, a, "y1b", 1)
                    variance(at, EPS1, "var3")
                    need(dve, a, "rstd3", 1)
                    scaled(at, at, "yn")
                if b is not None:
                    need(dve, b, "wo_ps", 1)
                    vv.tensor_tensor(res[:], x_in[:], tm["B"], ALU.add).then_inc(sem["x1"], 1)
                    need(dve, b, "x1", 1)
                    variance(res, EPS0, "var")
                    need(dve, b, "rstd", 3)
                    scaled(res, tok, "xn")
                    shift(b, 2)
                    mixed(xa, "ffn_maa_k", "xk")
                    mixed(xb, "ffn_maa_r", "xr")
                    need(dve, b, "rr", 1)
                    st.then(vv.tensor_scalar(rT_tm, rT_tm, 0.5, 0.5, ALU.mult, ALU.add))
                    need(dve, b, "fv_ps", 1)
                    st.then(vv.tensor_tensor(rT_tm, tm["A"], rT_tm, ALU.mult))
                    vv.tensor_tensor(res[:], res[:], rT_tm, ALU.add).then_inc(sem["x2"], 1)
                    need(dve, b, "q_hi", 1)
                    vv.tensor_tensor(rT[:].bitcast(F32R), xb, kT[:], ALU.subtract).then_inc(sem["q_lo"], 1)

            iterate(dve, body)

        @block.tensor
        def _(pe):
            mm = nc.tensor.matmul

            def features(out, w, x):
                for c in range(C):
                    for k in range(C):
                        ins = mm(out[:, c, :], w[:, k, c * P:(c + 1) * P], x[:, k, :], start=(k == 0), stop=(k == C - 1))
                return ins

            def tokens(out, x, w):
                for i in range(TT):
                    for k in range(C):
                        ins = mm(out[:, i, :], x[:, k, i * P:(i + 1) * P], w[:, k, :], start=(k == 0), stop=(k == C - 1))
                return ins

            def to_features(out, x):
                for i in range(TT):
                    for c in range(C):
                        ins = nc.tensor.transpose(out[:, c, i * P:(i + 1) * P], x[:, i, c * P:(c + 1) * P], ident[:])
                return ins

            def to_tokens(out, x):
                for i in range(TT):
                    for c in range(C):
                        ins = nc.tensor.transpose(out[:, i, c * P:(c + 1) * P], x[:, c, i * P:(i + 1) * P], ident[:])
                return ins

            def before(b):
                if isinstance(b, int) and b == 0:
                    pe.wait_ge(s_w1, 16 * N_EARLY)
                    pe.wait_ge(s_const, 1)
                need(pe, b, "xn", 1)
                to_features(fm["A"], tok).then_inc(sem["xT_ps"], 1)
                need(pe, b, "xm", 1)
                for k in range(C):
                    mm(ps[:, 2, 0:T], mw1[:, k, 0:P], xb[:, k, :], start=(k == 0), stop=(k == C - 1))
                for k in range(C):
                    ins = mm(ps[0:MAA, 3, 0:T], mw1[:, k, P:P + MAA], xb[:, k, :], start=(k == 0), stop=(k == C - 1))
                ins.then_inc(sem["m1_ps"], 1)

                def spread(j):
                    s = STREAMS[j]
                    if j >= 2:
                        need(pe, b, "x5m", j - 1)
                    for c in range(C):
                        ins = mm(fm["CD"[j % 2]][:, c, :], mw2[:, s // 4, c * P:(c + 1) * P], th[:, s, :], start=True, stop=True)
                    ins.then_inc(sem["w2_ps"], 1)

                need(pe, b, "th", 1)
                spread(0)
                for j in range(5):
                    if j < 4:
                        spread(j + 1)
                    if j == RS and isinstance(b, int) and b == 0:
                        pe.wait_ge(s_w2, 16 * N_LATE)
                    need(pe, b, "x5", j + 1)
                    if j >= 2:
                        need(pe, b, "proj", j - 1)
                    if j == GS:
                        need(pe, b, "proj", WS + 1)
                    x5, out = (xa, xb)[j % 2], fm["AB"[j % 2]]
                    if j == WS:
                        for k in range(C):
                            ins = mm(ps[0:DEC, 0, 0:T], dw1[:, k, :], x5[:, k, :], start=(k == 0), stop=(k == C - 1))
                        ins.then_inc(sem["proj_ps"], 1)
                        need(pe, b, "hid", 1)
                        for c in range(C):
                            ins = mm(fm["A"][:, c, :], dw2[:, c * P:(c + 1) * P], hid[:], start=True, stop=True)
                        ins.then_inc(sem["z_ps"], 1)
                    else:
                        features(out, W[{VS: "WvT", KS: "WkT", RS: "WrT", GS: "WgT"}[j]], x5).then_inc(sem["proj_ps"], 1)
                need(pe, b, "ruk", 1)
                for c in range(C):
                    ins = mm(fm["B"][:, c, :], hones[:], tok_fm[:, c, :], start=True, stop=True)
                ins.then_inc(sem["bonus_ps"], 1)

            def reduce(b, u):
                c, q = divmod(u, NQ)
                need(pe, b, "y", u + 1)
                if q == 0:
                    need(pe, b, "att", c)
                for k in range(DH):
                    dd = q * DH + k
                    ins = mm(ps[:, 4, (c % 2) * T:(c % 2) * T + T], pick[:, HS - 1 - dd:HS - 1 - dd + P],
                             AB[:, u % NAB, k, :], start=(dd == 0), stop=(dd == HS - 1))
                ins.then_inc(sem["red"], 1)

            def scores(a, i):
                qt, kv = divmod(i, KVH)
                need(pe, a, "neg", i - 1)
                for h in range(2):
                    ins = mm(tm["AB"[i % 2]][:, h, :], Q4[:, 2 * kv + h, qt * P:(qt + 1) * P],
                             K4[:, kv, :, :].rearrange("p a t -> p (a t)"), start=True, stop=True)
                ins.then_inc(sem["sc_ps"], 1)

            def attention(a, i):
                if 1 <= i <= AUNITS:
                    need(pe, a, "pr", i)
                    need(pe, a, "pt", i - 1)
                    for t in range(2):
                        for h in range(GRP):
                            ins = nc.tensor.transpose(ps[:, 6 + t, h * P:(h + 1) * P],
                                                      SM[:, (i - 1) % 2, h, t * P:(t + 1) * P], ident[:])
                    ins.then_inc(sem["pt_ps"], 1)
                if i >= 3 and (i - 3) % 4 == 3:
                    need(pe, a, "ot", (i - 3) // 4 + 1)
                    for h in range(GRP):
                        ins = nc.tensor.transpose(ps[:, 5, h * P:(h + 1) * P], OT[:, h * P:(h + 1) * P], ident[:])
                    ins.then_inc(sem["ot_ps"], 1)
                if 2 <= i < AUNITS + 2:
                    kv = (i - 2) % KVH
                    need(pe, a, "pt", i - 1)
                    if kv % 4 == 0:
                        need(pe, a, "ot2", (i - 2) // 4)
                    at_ = 32 * (kv % 4)
                    for t in range(2):
                        ins = mm(ps[at_:at_ + 32, 5, :], vaug[:, t, kv, :], PT[:, t, :], start=(t == 0), stop=(t == 1))
                    ins.then_inc(sem["pv"], 1)

            def body(b, a):
                if b is not None:
                    before(b)
                if a is not None:
                    need(pe, a, "k4_in", 128)
                    need(pe, a, "q4_in", 128)
                    if b is not None:
                        need(pe, b, "bonus", 1)
                    scores(a, 0)
                for i in range(STEPS):
                    if a is not None and i + 1 < AUNITS:
                        scores(a, i + 1)
                    if b is not None and 1 <= i <= UNITS:
                        reduce(b, i - 1)
                    if a is not None:
                        attention(a, i)
                if b is not None:
                    need(pe, b, "att", C)
                    to_tokens(tm["D"], tok_fm).then_inc(sem["att_ps"], 1)
                if a is not None:
                    need(pe, a, "at", SETS)
                    to_features(fm["A"], at).then_inc(sem["oT_ps"], 1)
                    need(pe, a, "oT", 1)
                    tokens(tm["B"], xb, W["Wo1"]).then_inc(sem["wo1_ps"], 1)
                if b is not None:
                    need(pe, b, "ctx_in", 16)
                    for k in range(C):
                        ins = mm(ps[:, 4, 0:T], Wk1[:, k, :], rT[:, k, :], start=(k == 0), stop=(k == C - 1))
                    ins.then_inc(sem["k_ps"], 1)
                    for i in range(TT):
                        for k in range(C):
                            ins = mm(ps[:, 5, i * P:(i + 1) * P], rT[:, k, i * P:(i + 1) * P], Wv1[:, k, :],
                                     start=(k == 0), stop=(k == C - 1))
                    ins.then_inc(sem["v_ps"], 1)
                    need(pe, b, "cenr", 1)
                    to_features(fm["A"], kT_tm).then_inc(sem["aT_ps"], 1)
                    need(pe, b, "attg", 1)
                    tokens(tm["B"], xa, W["WoT"]).then_inc(sem["wo_ps"], 1)
                    need(pe, b, "xn", 2)
                    to_features(fm["A"], tok).then_inc(sem["xT_ps"], 1)
                    need(pe, b, "xk", 1)
                    features(fm["C"], W["fWkT"], xa).then_inc(sem["kk_ps"], 1)
                    need(pe, b, "xr", 1)
                    tokens(tm["D"], xb, W["fWrT"]).then_inc(sem["rr_ps"], 1)
                    need(pe, b, "kk", 1)
                    tokens(tm["A"], kT, W["fWvT"]).then_inc(sem["fv_ps"], 1)
                    need(pe, b, "x2", 1)
                    to_features(fm["B"], res).then_inc(sem["x2T_ps"], 1)
                    need(pe, b, "x2T", 1)
                    features(fm["C"], W["Wq"], xa).then_inc(sem["q_ps"], 1)

            iterate(pe, body)


def kernel(**inputs):
    import numpy as np
    import concourse.bacc as bacc
    from concourse.bass_utils import run_bass_kernel_spmd as run

    a = {n: np.asarray(v) for n, v in inputs.items()}
    L0, L1 = "L0_xattn_", "L1_xattn_"

    def chunks(w):
        return np.ascontiguousarray(w.reshape(C, P, -1).transpose(1, 0, 2))

    arrays = {
        "x": np.ascontiguousarray(a["x"].reshape(B, TT, P, E).transpose(0, 2, 1, 3)),
        "prev": np.ascontiguousarray(a["ctx_2048"][:, 0:2].reshape(B, 2, C, P).transpose(0, 3, 2, 1)),
        "ctxT": np.ascontiguousarray(a["ctx_2048"].reshape(B, T, C, P).transpose(0, 3, 2, 1)),
        "s0": np.ascontiguousarray(a["ctx_2048"][:, 2:2 + HS].reshape(B, C, P, HS).transpose(0, 2, 1, 3)),
        "mask": np.ascontiguousarray(a["mask_Bx1xSxS2_ff0"].reshape(B, TT, P, T).transpose(0, 2, 1, 3)),
        "mw1": chunks(a[L0 + "maa_w1"]),
        "dw1": chunks(a[L0 + "decay_w1"]),
        "dw2": np.concatenate([a[L0 + "decay_w2"], np.zeros((P - DEC, E), np.float32)]),
        "bv": a[L1 + "bv"],
        "bo": a[L1 + "bo"], "gamma": a[L1 + "gamma"], "beta": a[L1 + "beta"],
    }
    w2 = np.zeros((P, 2, E), np.float32)
    w2[:, 0] = a[L0 + "maa_w2"][0:4].reshape(P, E)
    w2[0:MAA, 1] = a[L0 + "maa_w2"][4]
    arrays["mw2"] = w2
    for n, k in (("WrT", "Wr"), ("WkT", "Wk"), ("WvT", "Wv"), ("WgT", "Wg"), ("WoT", "Wo"),
                 ("fWkT", "ffn_Wk"), ("fWrT", "ffn_Wr"), ("fWvT", "ffn_Wv")):
        arrays[n] = chunks(a[L0 + k].T)
    for n, k in (("Wq", "Wq"), ("Wk1", "Wk"), ("Wv1", "Wv"), ("Wo1", "Wo")):
        arrays[n] = chunks(a[L1 + k])
    flat = {"bq": a[L1 + "bq"], "faaaa": a[L0 + "faaaa"].reshape(E)}
    for s in range(5):
        flat[f"stack{s}"] = a[L0 + "maa_stack"][s]
    cols = [flat[n] if n in flat else a[L0 + n] for n in VECS]
    arrays["vec"] = np.ascontiguousarray(
        np.concatenate([v.reshape(C, P) for v in cols] + [a[L1 + "bk"].reshape(1, P)]).T)

    nc = bacc.Bacc("TRN2", target_bir_lowering=False, num_devices=1, dynamic_dma_scratch_size=2048)
    d = {n: nc.dram_tensor("in_" + n, v.shape, F32, kind="ExternalInput").ap() for n, v in arrays.items()}
    d["out"] = nc.dram_tensor("out_y", (B, P, TT, E), F32, kind="ExternalOutput").ap()
    build(nc, d)
    r = run(nc, [{"in_" + n: v for n, v in arrays.items()}], core_ids=[0])
    y = np.asarray(r.results[0]["out_y"])
    return np.ascontiguousarray(y.reshape(B, P, TT, E).transpose(0, 2, 1, 3).reshape(B, T, E))
```

```python
from contextlib import ExitStack

import concourse.bass as bass
from concourse import mybir

F32 = mybir.dt.float32
F32R = mybir.dt.float32r
ALU = mybir.AluOpType
ACT = mybir.ActivationFunctionType
AX = mybir.AxisListType

B, T, E = 8, 256, 512
H, HS = 32, 16
KVH = 8
P = 128
C = E // P
TT = T // P
MAA, DEC = 32, 64
EPS0, EPS1 = 1e-5, 1e-6
N_FIRST, N_EARLY, N_LATE = 3, 7, 14
QSCALE = HS ** -0.5
STREAMS = [2, 0, 1, 3, 4]
VS, KS, WS, RS, GS = range(5)
DH = 4
DL = {True: 1, False: 2}
NQ = HS // DH
UNITS = NQ * C
NAB = 3
AUNITS = TT * KVH
GRP = H // KVH
SETS = AUNITS // 4
STEPS = AUNITS + 4

VECS = ["gn_w", "gn_b", "ln1_w", "ln1_b", "ln2_w", "ln2_b", "maa_x", "stack0", "stack1", "stack2", "stack3", "stack4",
        "time_decay", "faaaa", "ffn_maa_k", "ffn_maa_r", "bq"]
NVEC = len(VECS) * C + 1
BK_COL = len(VECS) * C

PER = dict(
    s0_in=16, prev_in=16, x_in=16, ctx_in=16, k_out=16, k4_in=128, v_out=16,
    vb0_in=96, vb1_in=80, vb2_in=80, mask_in=16, q_hi_out=16, q_lo_out=16, q4_in=128, y_out=16,
    k_ps=1, v_ps=1, k_hi=1, k_lo=1, v_aug=1,
    var=2 * TT, rstd=2 * TT, xn=2 * TT, xT_ps=2, xnT=2 * C, xm=C, m1_ps=2, th=5,
    w2_ps=10, x5m=5, x5=5, x5_high=1, proj_ps=5, hid=1, z_ps=1, proj=5, gate=1,
    ruk=1, bonus_ps=1, bonus=1, kv=UNITS, scan=2 * UNITS, y=UNITS, y_low=UNITS, red=UNITS, att=C,
    att_ps=TT, cen=TT, sq=TT, gn_var=TT, gn_dev=TT, cenr=TT, aT_ps=1, aT=C, attg=1, wo_ps=TT, x1=1,
    xk=1, xr=1, kk_ps=1, relu=1, kk=1, rr_ps=1, rr=1, fv_ps=TT, x2=TT,
    x2T_ps=1, x2T=1, x2T_high=1, q_ps=1, q_hi=1, q_lo=1,
    sc_ps=AUNITS, neg=AUNITS, pr=AUNITS, pt_ps=AUNITS, pt=AUNITS, pv=AUNITS,
    ot=SETS, ot_ps=SETS, ot2=SETS, at=SETS,
    oT_ps=1, oT=1, wo1_ps=1, res_b=1, y1=1, var3=1, rstd3=1, yn=1, y_done=1,
)


def build(nc, d):
    ctx = ExitStack()
    with ctx:
        def sb(name, shape, dt=F32, where=ctx):
            return where.enter_context(nc.sbuf_tensor(name, shape, dt))

        big = ["WrT", "WkT", "WvT", "WgT", "WoT", "fWkT", "fWrT", "fWvT", "Wq", "Wo1"]
        W = {n: sb(n, [P, C, E]) for n in big}
        Wk1, Wv1 = sb("Wk1", [P, C, P]), sb("Wv1", [P, C, P])
        mw1 = sb("mw1", [P, C, 5 * MAA])
        mw2 = sb("mw2", [P, 2, E])
        dw1 = sb("dw1", [P, C, DEC])
        dw2 = sb("dw2", [P, E])
        vec = sb("vec", [P, NVEC])
        rows = sb("rows", [P, 3, E])
        bv_r = sb("bv_r", [P, P])
        ident = sb("ident", [P, P])
        pick = sb("pick", [P, P + HS])
        hones = sb("hones", [P, P])
        bq4 = sb("bq4", [P, C])
        gn_half = sb("gn_half", [P, 2 * C])
        spare = sb("spare", [P, 1])
        half = sb("half", [P, TT])

        x_in = sb("x_in_t", [P, TT, E])
        res = sb("res", [P, TT, E])
        tok = sb("tok", [P, TT, E])
        xnT = sb("xnT_t", [P, C, T + 1])
        sx = sb("sx_t", [P, C, T])
        mask = sx[:, 0:2, :]
        OT = sx[:, 2:4, :].rearrange("p a t -> p (a t)")
        xab = sb("xab", [P, 2, C, T])
        xa, xb, SM = xab[:, 0, :, :], xab[:, 1, :, :], xab
        kT, vT, rT, wT = (sb(n, [P, C, T]) for n in ("kT", "vT", "rT", "wT"))
        g = sb("g", [P, C, T])
        at = sb("at_t", [P, TT, E])
        th = sb("th_t", [P, 5, T])
        hid = sb("hid_t", [P, T])
        s0 = sb("s0", [P, C, HS])
        prev = sb("prev", [P, C, 2])
        vaug = sb("vaug_t", [P, TT, KVH, 2 * HS])
        K4 = sb("K4", [P, KVH, 2, T], F32R)
        stat = sb("stat", [P, TT, 6])
        mv = sb("mv", [P, TT, 2])
        ve = sb("ve", [P, 2 * H])
        rs = sb("rs", [P, 2 * H])
        mean = sb("mean", [P, 2 * H])
        nmax = sb("nmax", [P, 2, GRP])
        rc = sb("rc", [P, GRP, 4])
        AB = sb("AB", [P, NAB, DH, T])
        S = sb("S", [P, 2, DH, T])
        Q4 = sb("Q4", [P, H // 2, T], F32R)
        PT = sb("PT", [P, 2, E])

        ps = ctx.enter_context(nc.psum_tensor("ps", [P, 8, 512], F32))
        tm = {n: ps[:, 2 * i:2 * i + 2, :] for i, n in enumerate("ABCD")}
        fm = {n: a.rearrange("p k (a t) -> p (k a) t", a=2) for n, a in tm.items()}

        kT_tm, rT_tm = (a[:].rearrange("p (i a) t -> p i (a t)", i=TT) for a in (kT, rT))
        tok_fm = tok[:].rearrange("p i (a t) -> p (i a) t", t=T)

        kscr = nc.dram_tensor("k_scratch", (2, P, T), F32, kind="Internal").ap()
        vscr = nc.dram_tensor("v_scratch", (E, T), F32, kind="Internal").ap()
        qscr = nc.dram_tensor("q_scratch", (2, E, T), F32, kind="Internal").ap()

        sem = {n: ctx.enter_context(nc.semaphore("s_" + n)) for n in PER}
        s_w0, s_w1, s_w2, s_const, s_seen, s_bq4, s_cst, s_past = (
            ctx.enter_context(nc.semaphore(n))
            for n in ("w_first", "w_early", "w_late", "consts", "seen", "bq4_done", "pool_const", "past"))
        s_v, s_p, s_a = (ctx.enter_context(nc.semaphore(n)) for n in ("vector_step", "pool_step", "scalar_step"))

        def tile_heads(x, i):
            return x[:, i * H:(i + 1) * H]

        def vcol(name, c):
            i = VECS.index(name) * C + c
            return vec[:, i:i + 1]

        def count(b, name, k):
            return b * PER[name] + k

        def past(b, name, k):
            v = count(b, name, k)
            return not isinstance(v, int) or v > 0

        class Steps:

            def __init__(self, eng, s):
                self.eng, self.s, self.n = eng, s, 0

            def start(self):
                if self.n:
                    self.eng.sem_inc(s_past, 1)
                    self.eng.sem_clear(self.s)
                self.n = 0

            def did(self, ins):
                ins.then_inc(self.s, 1)
                self.n += 1

            def wait(self, but=0):
                self.eng.wait_ge(self.s, self.n - but)

            def then(self, ins):
                self.did(ins)
                self.wait()

        def iterate(eng, body):
            body(0, None)
            body(1, 0)
            with eng.Fori(2, B) as b:
                body(b, b - 1)
            body(None, B - 1)

        block = ctx.enter_context(nc.Block())

        @block.sync
        def _(sp):
            early = [(vec[:], d["vec"]), (mw1[:], d["mw1"]), (mw2[:], d["mw2"]), (W["WvT"][:], d["WvT"]),
                     (W["WkT"][:], d["WkT"]), (dw1[:], d["dw1"]), (dw2[:], d["dw2"])]
            late = [(W[n][:], d[n]) for n in ("WrT", "WgT", "WoT", "fWkT", "fWrT", "fWvT", "Wq", "Wo1")]
            late += [(Wk1[:], d["Wk1"]), (Wv1[:], d["Wv1"]),
                     (bv_r[:], d["bv"].rearrange("(a n) -> a n", a=1).to_broadcast([P, P]))]
            late += [(rows[:, i, :], d[n].rearrange("(a n) -> a n", a=1).to_broadcast([P, E]))
                     for i, n in enumerate(("bo", "gamma", "beta"))]
            assert len(early) == N_EARLY and len(late) == N_LATE

            def alone():
                sp.sem_inc(s_past, 1)

            def unit_in(b, u):
                c, q = divmod(u, NQ)
                if u >= NAB:
                    if past(b, "scan", 2 * (u - NAB + 1)):
                        sp.wait_ge(sem["scan"], count(b, "scan", 2 * (u - NAB + 1)))
                        alone()
                src = vscr[c * P:(c + 1) * P, :].rearrange("(h e d) t -> h e (d t)", e=NQ, d=DH)[:, q, :]
                sp.dma_start(AB[:, u % NAB, :, :].rearrange("p d t -> p (d t)"),
                             src.unsqueeze(1).to_broadcast([P // HS, HS, DH * T])
                             ).then_inc(sem[f"vb{u % NAB}_in"], 16)

            def body(b, a):
                if b is not None:
                    if past(b, "x1", 0):
                        sp.wait_ge(sem["x1"], count(b, "x1", 0))
                        alone()
                    sp.dma_start(x_in[:], d["x"][b]).then_inc(sem["x_in"], 16)
                    if past(b, "xnT", 0):
                        sp.wait_ge(sem["xnT"], count(b, "xnT", 0))
                        alone()
                    sp.dma_start(prev[:], d["prev"][b]).then_inc(sem["prev_in"], 16)
                    if past(b, "y", 0):
                        sp.wait_ge(sem["y"], count(b, "y", 0))
                        alone()
                    sp.dma_start(s0[:], d["s0"][b]).then_inc(sem["s0_in"], 16)
                    if isinstance(b, int) and b == 0:
                        for n, (dst, src) in enumerate(early):
                            sp.dma_start(dst, src).then_inc(s_w0 if n < N_FIRST else s_w1, 16)
                        for dst, src in late:
                            sp.dma_start(dst, src).then_inc(s_w2, 16)
                if a is not None:
                    for part, (signal, src) in enumerate((("q_hi", kT), ("q_lo", rT))):
                        if past(a, "q4_in", 0):
                            sp.wait_ge(sem["q4_in"], count(a, "q4_in", 0))
                            alone()
                        sp.wait_ge(sem[signal], count(a, signal, 1))
                        alone()
                        out = signal + "_out"
                        sp.dma_start(qscr[part].rearrange("(c p) t -> p c t", p=P), src[:]).then_inc(sem[out], 16)
                    for part, out in enumerate(("q_hi_out", "q_lo_out")):
                        sp.wait_ge(sem[out], count(a, out, 16))
                        alone()
                        if past(a, "sc_ps", 0):
                            sp.wait_ge(sem["sc_ps"], count(a, "sc_ps", 0))
                            alone()
                        for h2 in range(2):
                            for again in range(2):
                                at_ = h2 * 64 + part * 32 + again * 16
                                src = qscr[part].rearrange("(p h k) t -> h k p t", h=2, k=HS)[h2]
                                sp.dma_start(Q4[at_:at_ + 16, :, :].bitcast(F32), src).then_inc(sem["q4_in"], 16)
                if b is not None:
                    sp.wait_ge(sem["proj"], count(b, "proj", VS + 1))
                    alone()
                    if past(b, "scan", 0):
                        sp.wait_ge(sem["scan"], count(b, "scan", 0))
                        alone()
                    sp.dma_start(vscr.rearrange("(c p) t -> p c t", p=P), vT[:]).then_inc(sem["v_out"], 16)
                    sp.wait_ge(sem["v_out"], count(b, "v_out", 16))
                    alone()
                    for u in range(NAB):
                        unit_in(b, u)
                if a is not None:
                    if b is not None:
                        sp.wait_ge(sem["x5m"], count(b, "x5m", 5))
                        alone()
                    sp.dma_start(mask, d["mask"][a]).then_inc(sem["mask_in"], 16)
                if b is not None:
                    for u in range(NAB, UNITS):
                        unit_in(b, u)
                    sp.wait_ge(sem["y"], count(b, "y", UNITS))
                    alone()
                    sp.wait_ge(sem["y_low"], count(b, "y_low", UNITS))
                    alone()
                    sp.dma_start(rT[:], d["ctxT"][b]).then_inc(sem["ctx_in"], 16)
                    sp.wait_ge(sem["k_hi"], count(b, "k_hi", 1))
                    alone()
                    sp.wait_ge(sem["k_lo"], count(b, "k_lo", 1))
                    alone()
                    if past(b, "k4_in", 0):
                        sp.wait_ge(sem["k4_in"], count(b, "k4_in", 0))
                        alone()
                    sp.dma_start(kscr.rearrange("a p t -> p a t"), wT[:, 1:3, :]).then_inc(sem["k_out"], 16)
                    sp.wait_ge(sem["k_out"], count(b, "k_out", 16))
                    alone()
                    if a is not None:
                        sp.wait_ge(sem["sc_ps"], count(a, "sc_ps", AUNITS))
                        alone()
                    else:
                        sp.wait_ge(s_const, 1)
                    for h2 in range(2):
                        for part in range(4):
                            at_ = h2 * 64 + part * 16
                            sp.dma_start(K4[at_:at_ + 16, :, h2, :].bitcast(F32),
                                         kscr[part % 2].rearrange("(g k) t -> k g t", k=HS)).then_inc(sem["k4_in"], 16)
                if a is not None:
                    sp.wait_ge(sem["y_done"], count(a, "y_done", 1))
                    alone()
                    sp.dma_start(d["out"][a], at[:]).then_inc(sem["y_out"], 16)

            iterate(sp, body)
            sp.wait_ge(sem["q4_in"], B * PER["q4_in"])
            sp.wait_ge(sem["y_out"], B * PER["y_out"])

        @block.gpsimd
        def _(pool):
            gp = nc.gpsimd
            st = Steps(pool, s_p)
            n = [0]

            def const(ins):
                n[0] += 1
                ins.then_inc(s_cst, 1)

            const(gp.memset(ident[:], 0.0))
            const(gp.memset(pick[:], 0.0))
            const(gp.memset(hones[:], 1.0))
            const(gp.memset(half[:], -0.5))
            pool.wait_ge(s_cst, n[0])
            heads = pick[:, HS - 1:HS - 1 + P].rearrange("p (h j) -> p h j", j=HS)[:, :, 0]
            const(gp.affine_select(out=ident[:], in_=ident[:], compare_op=ALU.not_equal, fill=1.0, base=0,
                                   pattern=[[-1, P]], channel_multiplier=1))
            const(gp.memset(heads, 1.0))
            pool.wait_ge(s_cst, n[0])
            nh = P // HS
            h3 = hones[:].rearrange("p (h j) -> p h j", j=HS)
            const(gp.affine_select(out=heads, in_=heads, compare_op=ALU.is_ge, fill=0.0, base=0,
                                   pattern=[[-HS, nh]], channel_multiplier=1))
            const(gp.affine_select(out=h3, in_=h3, compare_op=ALU.is_ge, fill=0.0, base=0,
                                   pattern=[[-HS, nh], [0, HS]], channel_multiplier=1))
            pool.wait_ge(s_cst, n[0])
            const(gp.affine_select(out=heads, in_=heads, compare_op=ALU.is_ge, fill=0.0, base=HS - 1,
                                   pattern=[[HS, nh]], channel_multiplier=-1))
            const(gp.affine_select(out=h3, in_=h3, compare_op=ALU.is_ge, fill=0.0, base=HS - 1,
                                   pattern=[[HS, nh], [0, HS]], channel_multiplier=-1))
            const(gp.memset(th[:], 0.0))
            const(gp.memset(hid[:], 0.0))
            const(gp.memset(vaug[:], 1.0))
            const(gp.memset(K4[:].bitcast(F32), 0.0))
            pool.wait_ge(s_cst, n[0])
            pool.sem_inc(s_const, 1)

            def rsqrt(b, i, n, k, var="var", rstd="rstd"):
                pool.wait_ge(sem[var], count(b, var, k))
                gp.tensor_tensor(rs[:, i:i + n], ve[:, i:i + n], half[:, 0:n], ALU.pow).then_inc(sem[rstd], 1)

            def row(i):
                return rows[:, i:i + 1, :].to_broadcast([P, TT, E])

            def body(b, a):
                st.start()
                if b is not None:
                    for i in range(TT):
                        rsqrt(b, i, 1, i + 1)
                    for j in range(5):
                        x5 = (xa, xb)[j % 2]
                        pool.wait_ge(sem["x5m"], count(b, "x5m", j + 1))
                        part = slice(0, C if j else C // 2)
                        gp.tensor_tensor(x5[:, part, :], x5[:, part, :], xnT[:, part, 1:T + 1],
                                         ALU.add).then_inc(sem["x5"], 1)
                    dl = DL[a is None]
                    pool.wait_ge(sem["proj"], count(b, "proj", KS + 1))
                    for u in range(UNITS + 1):
                        if u < UNITS:
                            pool.wait_ge(sem[f"vb{u % NAB}_in"], count(b, f"vb{u % NAB}_in", 16 * (u // NAB + 1)))
                            ab, c = AB[:, u % NAB, :, :], u // NQ
                            gp.tensor_tensor(ab, ab, kT[:, c:c + 1, :].to_broadcast([P, DH, T]),
                                             ALU.mult).then_inc(sem["kv"], 1)
                        if u >= 1:
                            if u == 1:
                                pool.wait_ge(sem["proj"], count(b, "proj", RS + 1))
                            pool.wait_ge(sem["scan"], count(b, "scan", 2 * u))
                            state, c = S[:, (u - 1) % 2, 0:dl, :], (u - 1) // NQ
                            gp.tensor_tensor(state, state, rT[:, c:c + 1, :].to_broadcast([P, dl, T]),
                                             ALU.mult).then_inc(sem["y_low"], 1)
                if a is not None:
                    pool.wait_ge(sem["oT_ps"], count(a, "oT_ps", 1))
                    gp.tensor_tensor(at[:], res[:], row(0), ALU.add).then_inc(sem["res_b"], 1)
                if b is not None:
                    for i in range(TT):
                        rsqrt(b, i, 1, TT + i + 1)
                if a is not None:
                    rsqrt(a, 0, TT, 1, "var3", "rstd3")
                if b is not None:
                    pool.wait_ge(sem["relu"], count(b, "relu", 1))
                    gp.tensor_tensor(kT[:], kT[:], kT[:], ALU.mult).then_inc(sem["kk"], 1)
                if a is not None:
                    pool.wait_ge(sem["yn"], count(a, "yn", 1))
                    st.then(gp.tensor_tensor(at[:], at[:], row(1), ALU.mult))
                    gp.tensor_tensor(at[:], at[:], row(2), ALU.add).then_inc(sem["y_done"], 1)

            iterate(pool, body)

        @block.scalar
        def _(act):
            sc = nc.scalar
            st = Steps(act, s_a)

            def shifted(b, k, src, w, bias, col):
                act.wait_ge(sem["xT_ps"], count(b, "xT_ps", k))
                sc.copy(xnT[:, :, 0:1], col)
                for c in range(C):
                    sc.activation(xnT[:, c, 1:T + 1], src[:, c, :], ACT.Identity, bias=vcol(bias, c),
                                  scale=vcol(w, c)).then_inc(sem["xnT"], 1)

            def queries(a):
                act.wait_ge(sem["q_ps"], count(a, "q_ps", 1))
                act.wait_ge(s_bq4, 1)
                for c in range(C):
                    ins = sc.activation(vT[:, c, :], fm["D"][:, c, :], ACT.Identity, bias=bq4[:, c:c + 1], scale=QSCALE)
                st.then(ins)
                sc.copy(kT[:].bitcast(F32R), vT[:]).then_inc(sem["q_hi"], 1)

            def before(b, a):
                if isinstance(b, int) and b == 0:
                    act.wait_ge(s_w0, 16 * N_FIRST)
                    for c in range(C):
                        ins = sc.mul(bq4[:, c:c + 1], vcol("bq", c), QSCALE)
                    assert VECS[0:2] == ["gn_w", "gn_b"]
                    ins = sc.mul(gn_half[:], vec[:, 0:2 * C], 0.5)
                    ins.then_inc(s_bq4, 1)
                act.wait_ge(sem["prev_in"], count(b, "prev_in", 16))
                shifted(b, 1, fm["A"], "ln1_w", "ln1_b", prev[:, :, 1:2])
                if a is not None:
                    queries(a)
                act.wait_ge(sem["m1_ps"], count(b, "m1_ps", 1))
                if isinstance(b, int) and b == 0:
                    act.wait_ge(s_const, 1)
                for s in STREAMS:
                    if s == 4:
                        act.wait_ge(sem["m1_ps"], count(b, "m1_ps", 2))
                    p = MAA * (s % 4)
                    sc.activation(th[p:p + MAA, s, :], ps[p:p + MAA, 2 + s // 4, 0:T], ACT.Tanh).then_inc(sem["th"], 1)
                act.wait_ge(sem["proj_ps"], count(b, "proj_ps", VS + 1))
                if a is not None:
                    act.wait_ge(sem["q_lo"], count(a, "q_lo", 1))
                sc.copy(vT[:], fm["A"]).then_inc(sem["proj"], 1)
                act.wait_ge(sem["proj_ps"], count(b, "proj_ps", KS + 1))
                if past(b, "q_hi_out", 0):
                    act.wait_ge(sem["q_hi_out"], count(b, "q_hi_out", 0))
                sc.copy(kT[:], fm["B"]).then_inc(sem["proj"], 1)
                act.wait_ge(sem["proj_ps"], count(b, "proj_ps", WS + 1))
                sc.activation(hid[0:DEC, :], ps[0:DEC, 0, 0:T], ACT.Tanh).then_inc(sem["hid"], 1)
                act.wait_ge(sem["z_ps"], count(b, "z_ps", 1))
                if past(b, "k_out", 0):
                    act.wait_ge(sem["k_out"], count(b, "k_out", 0))
                for c in range(C):
                    ins = sc.activation(wT[:, c, :], fm["A"][:, c, :], ACT.Exp, bias=vcol("time_decay", c))
                st.then(ins)
                sc.activation(wT[:], wT[:], ACT.Exp, scale=-1.0).then_inc(sem["proj"], 1)
                act.wait_ge(sem["proj_ps"], count(b, "proj_ps", RS + 1))
                if past(b, "q_lo_out", 0):
                    act.wait_ge(sem["q_lo_out"], count(b, "q_lo_out", 0))
                sc.copy(rT[:], fm["B"]).then_inc(sem["proj"], 1)
                if a is not None:
                    attention(a, 0)
                act.wait_ge(sem["proj_ps"], count(b, "proj_ps", GS + 1))
                sc.activation(g[:], fm["C"], ACT.Tanh, scale=0.5).then_inc(sem["proj"], 1)

            def attention(a, i):
                if 0 <= i - 3 < AUNITS and (i - 3) % 4 == 3:
                    act.wait_ge(sem["ot_ps"], count(a, "ot_ps", (i - 3) // 4 + 1))
                    sc.copy(OT, ps[:, 5, :]).then_inc(sem["ot2"], 1)
                if i < AUNITS:
                    act.wait_ge(sem["neg"], count(a, "neg", i + 1))
                    for h in range(GRP):
                        ins = sc.activation(SM[:, (i + 1) % 2, h, :], SM[:, (i + 1) % 2, h, :], ACT.Exp, scale=-1.0,
                                            bias=nmax[:, i % 2, h:h + 1])
                    ins.then_inc(sem["pr"], 1)
                if 1 <= i <= AUNITS:
                    act.wait_ge(sem["pt_ps"], count(a, "pt_ps", i))
                    if past(a, "pv", i - 1):
                        act.wait_ge(sem["pv"], count(a, "pv", i - 1))
                    sc.copy(PT[:], tm["D"]).then_inc(sem["pt"], 1)
                if 0 <= i - 2 < AUNITS and (i - 2) % 4 == 3:
                    if past(a, "pv", i - 1):
                        act.wait_ge(sem["pv"], count(a, "pv", i - 1))
                    if past(a, "at", (i - 2) // 4):
                        act.wait_ge(sem["at"], count(a, "at", (i - 2) // 4))
                    sc.copy(OT, ps[:, 5, :]).then_inc(sem["ot"], 1)

            def collect(b, c):
                act.wait_ge(sem["red"], count(b, "red", NQ * (c + 1)))
                sc.copy(tok_fm[:, c, :], ps[:, 4, (c % 2) * T:(c % 2) * T + T]).then_inc(sem["att"], 1)

            def body(b, a):
                st.start()
                if b is not None:
                    before(b, a)
                else:
                    queries(a)
                for i in range(0 if b is None else 1, STEPS):
                    if a is not None:
                        attention(a, i)
                    if b is not None and 1 <= i <= UNITS and i % NQ == 0:
                        collect(b, i // NQ - 1)
                    if b is not None and i == UNITS + 1:
                        sc.activation(spare[:], ident[:, 0:1], ACT.Sqrt)
                if b is not None:
                    act.wait_ge(sem["att_ps"], count(b, "att_ps", TT))
                    for i in range(TT):
                        act.wait_ge(sem["cen"], count(b, "cen", i + 1))
                        sc.activation(tok[:, i, :], kT_tm[:, i, :], ACT.Square).then_inc(sem["sq"], 1)
                if a is not None:
                    act.wait_ge(sem["oT_ps"], count(a, "oT_ps", 1))
                    sc.copy(xb, fm["C"]).then_inc(sem["oT"], 1)
                if b is not None:
                    for i in range(TT):
                        act.wait_ge(sem["gn_var"], count(b, "gn_var", i + 1))
                        sc.activation(tile_heads(ve, i), tile_heads(ve, i), ACT.Sqrt).then_inc(sem["gn_dev"], 1)
                    act.wait_ge(sem["aT_ps"], count(b, "aT_ps", 1))
                    act.wait_ge(s_bq4, 1)
                    for c in range(C):
                        sc.activation(xa[:, c, :], fm["A"][:, c, :], ACT.Identity, bias=gn_half[:, C + c:C + c + 1],
                                      scale=gn_half[:, c:c + 1]).then_inc(sem["aT"], 1)
                    act.wait_ge(sem["k_ps"], count(b, "k_ps", 1))
                    if isinstance(b, int) and b == 0:
                        act.wait_ge(s_w2, 16 * N_LATE)
                    st.then(sc.activation(wT[:, 0, :], ps[:, 2, 0:T], ACT.Identity, bias=vec[:, BK_COL:BK_COL + 1]))
                    sc.copy(wT[:, 1, :].bitcast(F32R), wT[:, 0, :]).then_inc(sem["k_hi"], 1)
                    shifted(b, 2, fm["A"], "ln2_w", "ln2_b", prev[:, :, 0:1])
                    act.wait_ge(sem["kk_ps"], count(b, "kk_ps", 1))
                    sc.activation(kT[:], fm["B"], ACT.Relu).then_inc(sem["relu"], 1)
                    act.wait_ge(sem["rr_ps"], count(b, "rr_ps", 1))
                    sc.activation(rT_tm, tm["D"], ACT.Tanh, scale=0.5).then_inc(sem["rr"], 1)
                    act.wait_ge(sem["x2T_ps"], count(b, "x2T_ps", 1))
                    sc.copy(xa[:, 0:C // 2, :], fm["A"][:, 0:C // 2, :]).then_inc(sem["x2T"], 1)

            iterate(act, body)

        @block.vector
        def _(dve):
            vv = nc.vector
            st = Steps(dve, s_v)

            def variance(src, eps, signal):
                for i in range(TT):
                    st.did(vv.bn_stats(stat[:, i, :], src[:, i, :]))
                st.wait()
                for i in range(TT):
                    st.did(vv.bn_aggr(mv[:, i, :], stat[:, i, :]))
                st.wait()
                vv.tensor_scalar(ve[:, 0:TT], mv[:, :, 1], eps, None, ALU.add).then_inc(sem[signal], 1)

            def scaled(src, out, signal):
                for i in range(TT):
                    ins = vv.tensor_scalar(out[:, i, :], src[:, i, :], mv[:, i, 0:1], rs[:, i:i + 1],
                                           ALU.subtract, ALU.mult)
                ins.then_inc(sem[signal], 1)

            def norm(b, k, x, tile):
                for i in range(TT):
                    tile(i)
                    st.then(vv.bn_stats(stat[:, i, :], x[:, i, :]))
                    st.then(vv.bn_aggr(mv[:, i, :], stat[:, i, :]))
                    vv.tensor_scalar(ve[:, i:i + 1], mv[:, i, 1:2], EPS0, None, ALU.add).then_inc(sem["var"], 1)
                for i in range(TT):
                    dve.wait_ge(sem["rstd"], count(b, "rstd", k * TT + i + 1))
                    vv.tensor_scalar(tok[:, i, :], x[:, i, :], mv[:, i, 0:1], rs[:, i:i + 1],
                                     ALU.subtract, ALU.mult).then_inc(sem["xn"], 1)

            def shift(b, k, c):
                dve.wait_ge(sem["xnT"], count(b, "xnT", k * C + c + 1))
                st.did(vv.tensor_tensor(sx[:, c, :], xnT[:, c, 0:T], xnT[:, c, 1:T + 1], ALU.subtract))

            def mixed(out, name, c):
                return vv.scalar_tensor_tensor(out=out[:, c, :], in0=sx[:, c, :], scalar=vcol(name, c),
                                               in1=xnT[:, c, 1:T + 1], op0=ALU.mult, op1=ALU.add)

            def shifts_and_mix(b, k, out, name):
                for c in range(C + 1):
                    if c < C:
                        shift(b, k, c)
                    if c >= 1:
                        st.wait(but=1 if c < C else 0)
                        ins = mixed(out, name, c - 1)
                        if k == 0:
                            ins.then_inc(sem["xm"], 1)
                return ins

            def queries_rest(b):
                dve.wait_ge(sem["q_hi"], count(b, "q_hi", 1))
                vv.tensor_tensor(rT[:].bitcast(F32R), vT[:], kT[:], ALU.subtract).then_inc(sem["q_lo"], 1)

            def before(b, a):
                dve.wait_ge(sem["x_in"], count(b, "x_in", 16))
                norm(b, 0, x_in, lambda i: None)
                if isinstance(b, int) and b == 0:
                    dve.wait_ge(s_w0, 16 * N_FIRST)
                shifts_and_mix(b, 0, xb, "maa_x")
                if a is not None:
                    queries_rest(a)
                for j, s in enumerate(STREAMS):
                    if past(b, "proj_ps", j - 1):
                        dve.wait_ge(sem["proj_ps"], count(b, "proj_ps", j - 1))
                    x5 = (xa, xb)[j % 2]
                    for c in range(C):
                        if c % 2 == 0:
                            dve.wait_ge(sem["w2_ps"], count(b, "w2_ps", 2 * j + c // 2 + 1))
                        ins = vv.scalar_tensor_tensor(out=x5[:, c, :], in0=fm["CD"[j % 2]][:, c, :],
                                                      scalar=vcol(f"stack{s}", c), in1=sx[:, c, :],
                                                      op0=ALU.add, op1=ALU.mult)
                    ins.then_inc(sem["x5m"], 1)
                    if j == 0:
                        dve.wait_ge(sem["x5m"], count(b, "x5m", 1))
                        high = slice(C // 2, C)
                        vv.tensor_tensor(x5[:, high, :], x5[:, high, :], xnT[:, high, 1:T + 1],
                                         ALU.add).then_inc(sem["x5_high"], 1)
                dve.wait_ge(sem["s0_in"], count(b, "s0_in", 16))
                dve.wait_ge(sem["proj"], count(b, "proj", WS + 1))
                recurrence(b, 0, DL[a is None])
                dve.wait_ge(sem["proj"], count(b, "proj", RS + 1))
                for c in range(C):
                    ins = vv.scalar_tensor_tensor(out=tok_fm[:, c, :], in0=rT[:, c, :], scalar=vcol("faaaa", c),
                                                  in1=kT[:, c, :], op0=ALU.mult, op1=ALU.mult)
                ins.then_inc(sem["ruk"], 1)

            def gates(b, a):
                dve.wait_ge(sem["bonus_ps"], count(b, "bonus_ps", 1))
                vv.tensor_tensor(tok_fm, fm["D"], vT[:], ALU.mult).then_inc(sem["bonus"], 1)
                recurrence(b, 1, DL[a is None])
                dve.wait_ge(sem["proj"], count(b, "proj", GS + 1))
                vv.scalar_tensor_tensor(out=g[:], in0=g[:], scalar=1.0, in1=fm["C"],
                                        op0=ALU.add, op1=ALU.mult).then_inc(sem["gate"], 1)

            def recurrence(b, u, dl):
                c, q = divmod(u, NQ)
                begin = s0[:, c, q * DH:q * DH + DH]
                if past(b, "red", u - 1):
                    dve.wait_ge(sem["red"], count(b, "red", u - 1))
                vv.tensor_copy(S[:, u % 2, :, 0], begin)
                dve.wait_ge(sem["kv"], count(b, "kv", u + 1))
                for part in (range(dl, DH), range(dl)):
                    for k in part:
                        ins = vv.tensor_tensor_scan(S[:, u % 2, k, 1:T], wT[:, c, 0:T - 1], AB[:, u % NAB, k, 0:T - 1],
                                                    begin[:, k:k + 1], ALU.mult, ALU.add)
                    ins.then_inc(sem["scan"], 1)

            def times_r(b, u, dl):
                c = u // NQ
                dve.wait_ge(sem["scan"], count(b, "scan", 2 * u + 1))
                state = S[:, u % 2, dl:DH, :]
                vv.tensor_tensor(state, state, rT[:, c:c + 1, :].to_broadcast([P, DH - dl, T]),
                                 ALU.mult).then_inc(sem["y"], 1)

            def by_head(x):
                return x.rearrange("p (h d) -> p h d", d=HS)

            def group_centre(b, i):
                att, m = by_head(tm["A"][:, i, :]), tile_heads(mean, i)
                dve.wait_ge(sem["att_ps"], count(b, "att_ps", i + 1))
                st.then(vv.tensor_reduce(m, att, AX.X, ALU.add))
                st.then(vv.tensor_scalar(m, m, 1.0 / HS, None, ALU.mult))
                vv.tensor_tensor(by_head(kT_tm[:, i, :]), att, m.unsqueeze(2).to_broadcast([P, H, HS]),
                                 ALU.subtract).then_inc(sem["cen"], 1)

            def group_scale(b):
                for i in range(TT):
                    v = tile_heads(ve, i)
                    dve.wait_ge(sem["sq"], count(b, "sq", i + 1))
                    st.then(vv.tensor_reduce(v, by_head(tok[:, i, :]), AX.X, ALU.add))
                    vv.tensor_scalar(v, v, 1.0 / HS, EPS0, ALU.mult, ALU.add).then_inc(sem["gn_var"], 1)
                for i in range(TT):
                    d1, cen = tile_heads(rs, i), by_head(kT_tm[:, i, :])
                    dve.wait_ge(sem["gn_dev"], count(b, "gn_dev", i + 1))
                    st.then(vv.reciprocal(d1, tile_heads(ve, i)))
                    vv.tensor_tensor(cen, cen, d1.unsqueeze(2).to_broadcast([P, H, HS]),
                                     ALU.mult).then_inc(sem["cenr"], 1)

            def attention(a, i):
                if i < AUNITS:
                    dve.wait_ge(sem["sc_ps"], count(a, "sc_ps", i + 1))
                    if past(a, "pt_ps", i - 1):
                        dve.wait_ge(sem["pt_ps"], count(a, "pt_ps", i - 1))
                    dve.sem_inc(s_seen, 1)
                    for h in range(GRP):
                        sps = tm["AB"[i % 2]][:, h // 2, (h % 2) * T:(h % 2) * T + T]
                        ins = vv.tensor_tensor_reduce(
                            out=SM[:, (i + 1) % 2, h, :], in0=sps, in1=mask[:, i // KVH, :], scale=-1.0,
                            scalar=3.0e38, op0=ALU.add, op1=ALU.min, accum_out=nmax[:, i % 2, h:h + 1])
                    ins.then_inc(sem["neg"], 1)
                if i >= 4 and (i - 4) % 4 == 3:
                    n = (i - 4) // 4
                    qt, gs = divmod(n, 2)
                    dve.wait_ge(sem["ot2"], count(a, "ot2", n + 1))
                    o = OT.rearrange("p (h g e) -> p h g e", h=GRP, g=4)
                    st.then(vv.reciprocal(rc[:], o[:, :, :, HS]))
                    vv.tensor_tensor(at[:, qt, gs * 256:gs * 256 + 256].rearrange("p (g h d) -> p h g d", g=4, h=GRP),
                                     o[:, :, :, 0:HS], rc[:].unsqueeze(3).to_broadcast([P, GRP, 4, HS]),
                                     ALU.mult).then_inc(sem["at"], 1)

            def body(b, a):
                st.start()
                if b is not None:
                    before(b, a)
                elif a is not None:
                    queries_rest(a)
                if a is not None:
                    dve.wait_ge(sem["mask_in"], count(a, "mask_in", 16))
                    if past(a, "y_out", 0):
                        dve.wait_ge(sem["y_out"], count(a, "y_out", 0))
                for i in range(STEPS):
                    if a is not None:
                        attention(a, i)
                    if b is not None:
                        if 2 <= i < UNITS:
                            recurrence(b, i, DL[a is None])
                        if i < UNITS:
                            times_r(b, i, DL[a is None])
                        if i == 0:
                            gates(b, a)
                        if i == UNITS + 1:
                            group_centre(b, 0)
                        if i == STEPS - 1:
                            group_centre(b, 1)
                if b is not None:
                    group_scale(b)
                    for c in range(C):
                        dve.wait_ge(sem["aT"], count(b, "aT", c + 1))
                        ins = vv.tensor_tensor(xa[:, c, :], xa[:, c, :], g[:, c, :], ALU.mult)
                    ins.then_inc(sem["attg"], 1)
                    if isinstance(b, int) and b == 0:
                        dve.wait_ge(s_w2, 16 * N_LATE)
                        dve.wait_ge(s_const, 1)
                    dve.wait_ge(sem["v_ps"], count(b, "v_ps", 1))
                    vv.tensor_tensor(vaug[:, :, :, 0:HS],
                                     ps[:, 3, 0:TT * P].rearrange("p (i g d) -> p i g d", i=TT, d=HS),
                                     bv_r[:].rearrange("p (i g d) -> p i g d", i=1, d=HS)
                                     .to_broadcast([P, TT, KVH, HS]),
                                     ALU.add).then_inc(sem["v_aug"], 1)
                    dve.wait_ge(sem["k_hi"], count(b, "k_hi", 1))
                    vv.tensor_tensor(wT[:, 2, :].bitcast(F32R), wT[:, 0, :], wT[:, 1, :],
                                     ALU.subtract).then_inc(sem["k_lo"], 1)
                    if a is not None:
                        dve.wait_ge(sem["res_b"], count(a, "res_b", 1))

                    def residual(i):
                        dve.wait_ge(sem["wo_ps"], count(b, "wo_ps", i + 1))
                        ins = vv.tensor_tensor(res[:, i, :], x_in[:, i, :], tm["C"][:, i, :], ALU.add)
                        if i == TT - 1:
                            ins.then_inc(sem["x1"], 1)
                            dve.wait_ge(sem["x1"], count(b, "x1", 1))
                        else:
                            st.then(ins)

                    norm(b, 1, res, residual)
                    shifts_and_mix(b, 1, xa, "ffn_maa_k").then_inc(sem["xk"], 1)
                    if a is not None:
                        dve.wait_ge(sem["wo1_ps"], count(a, "wo1_ps", 1))
                    for c in range(C):
                        ins = mixed(xb, "ffn_maa_r", c)
                    ins.then_inc(sem["xr"], 1)
                if a is not None:
                    dve.wait_ge(sem["wo1_ps"], count(a, "wo1_ps", 1))
                    dve.wait_ge(sem["res_b"], count(a, "res_b", 1))
                    vv.tensor_tensor(at[:], at[:], tm["D"], ALU.add).then_inc(sem["y1"], 1)
                    dve.wait_ge(sem["y1"], count(a, "y1", 1))
                    variance(at, EPS1, "var3")
                    dve.wait_ge(sem["rstd3"], count(a, "rstd3", 1))
                    scaled(at, at, "yn")
                if b is not None:
                    dve.wait_ge(sem["rr"], count(b, "rr", 1))
                    for i in range(TT):
                        dve.wait_ge(sem["fv_ps"], count(b, "fv_ps", i + 1))
                        st.then(vv.scalar_tensor_tensor(out=rT_tm[:, i, :], in0=rT_tm[:, i, :], scalar=1.0,
                                                        in1=tm["C"][:, i, :], op0=ALU.add, op1=ALU.mult))
                        vv.scalar_tensor_tensor(out=res[:, i, :], in0=rT_tm[:, i, :], scalar=0.5, in1=res[:, i, :],
                                                op0=ALU.mult, op1=ALU.add).then_inc(sem["x2"], 1)
                    dve.wait_ge(sem["x2T_ps"], count(b, "x2T_ps", 1))
                    vv.tensor_copy(xa[:, C // 2:C, :], fm["A"][:, C // 2:C, :]).then_inc(sem["x2T_high"], 1)

            iterate(dve, body)

        @block.tensor
        def _(pe):
            mm = nc.tensor.matmul

            def features(out, w, x, chunks=range(C)):
                for c in chunks:
                    for k in range(C):
                        ins = mm(out[:, c, :], w[:, k, c * P:(c + 1) * P], x[:, k, :],
                                 start=(k == 0), stop=(k == C - 1))
                return ins

            def tokens(out, x, w, each=None, tiles=range(TT)):
                for i in tiles:
                    for k in range(C):
                        ins = mm(out[:, i, :], x[:, k, i * P:(i + 1) * P], w[:, k, :],
                                 start=(k == 0), stop=(k == C - 1))
                    if each:
                        ins.then_inc(sem[each], 1)
                return ins

            def to_features(out, x, tiles=range(TT)):
                for i in tiles:
                    for c in range(C):
                        ins = nc.tensor.transpose(out[:, c, i * P:(i + 1) * P], x[:, i, c * P:(c + 1) * P], ident[:])
                return ins

            def norm_to_features(b, k, out):
                for i in range(TT):
                    pe.wait_ge(sem["xn"], count(b, "xn", k * TT + i + 1))
                    ins = to_features(out, tok, [i])
                ins.then_inc(sem["xT_ps"], 1)

            def to_tokens(out, x, tiles):
                for i in tiles:
                    for c in range(C):
                        ins = nc.tensor.transpose(out[:, i, c * P:(c + 1) * P], x[:, c, i * P:(i + 1) * P], ident[:])
                return ins

            def before(b, a):
                if isinstance(b, int) and b == 0:
                    pe.wait_ge(s_w0, 16 * N_FIRST)
                    pe.wait_ge(s_const, 1)
                norm_to_features(b, 0, fm["A"])
                for k in range(C):
                    pe.wait_ge(sem["xm"], count(b, "xm", k + 1))
                    ins = mm(ps[:, 2, 0:T], mw1[:, k, 0:P], xb[:, k, :], start=(k == 0), stop=(k == C - 1))
                ins.then_inc(sem["m1_ps"], 1)
                for k in range(C):
                    ins = mm(ps[0:MAA, 3, 0:T], mw1[:, k, P:P + MAA], xb[:, k, :], start=(k == 0), stop=(k == C - 1))
                ins.then_inc(sem["m1_ps"], 1)

                def spread(j):
                    s = STREAMS[j]
                    if j >= 2:
                        pe.wait_ge(sem["x5m"], count(b, "x5m", j - 1))
                    pe.wait_ge(sem["th"], count(b, "th", j + 1))
                    for c in range(C):
                        ins = mm(fm["CD"[j % 2]][:, c, :], mw2[:, s // 4, c * P:(c + 1) * P], th[:, s, :],
                                 start=True, stop=True)
                        if c % 2:
                            ins.then_inc(sem["w2_ps"], 1)

                spread(0)
                for j in range(5):
                    if j < 4:
                        spread(j + 1)
                    if j == RS and isinstance(b, int) and b == 0:
                        pe.wait_ge(s_w2, 16 * N_LATE)
                    pe.wait_ge(sem["x5"], count(b, "x5", j + 1))
                    if j == 0:
                        pe.wait_ge(sem["x5_high"], count(b, "x5_high", 1))
                        if isinstance(b, int) and b == 0:
                            pe.wait_ge(s_w1, 16 * (N_EARLY - N_FIRST))
                    if j == 1:
                        pe.wait_ge(sem["th"], count(b, "th", 5))
                    if j >= 2:
                        pe.wait_ge(sem["proj"], count(b, "proj", j - 1))
                    x5, out = (xa, xb)[j % 2], fm["ABABC"[j]]
                    if j == WS:
                        for k in range(C):
                            ins = mm(ps[0:DEC, 0, 0:T], dw1[:, k, :], x5[:, k, :], start=(k == 0), stop=(k == C - 1))
                        ins.then_inc(sem["proj_ps"], 1)
                        pe.wait_ge(sem["hid"], count(b, "hid", 1))
                        for c in range(C):
                            ins = mm(fm["A"][:, c, :], dw2[:, c * P:(c + 1) * P], hid[:], start=True, stop=True)
                        ins.then_inc(sem["z_ps"], 1)
                    elif j == GS:
                        features(out, W["WgT"], x5, range(C // 2))
                        if a is not None:
                            pe.wait_ge(sem["k4_in"], count(a, "k4_in", 128))
                            pe.wait_ge(sem["q4_in"], count(a, "q4_in", 128))
                            scores(a, 0)
                        pe.wait_ge(sem["ruk"], count(b, "ruk", 1))
                        for c in range(C):
                            ins = mm(fm["D"][:, c, :], hones[:], tok_fm[:, c, :], start=True, stop=True)
                        ins.then_inc(sem["bonus_ps"], 1)
                        features(out, W["WgT"], x5, range(C // 2, C)).then_inc(sem["proj_ps"], 1)
                    else:
                        weight = W[{VS: "WvT", KS: "WkT", RS: "WrT"}[j]]
                        features(out, weight, x5).then_inc(sem["proj_ps"], 1)

            def reduce(b, u):
                c, q = divmod(u, NQ)
                pe.wait_ge(sem["y"], count(b, "y", u + 1))
                pe.wait_ge(sem["y_low"], count(b, "y_low", u + 1))
                if q == 0:
                    if past(b, "att", c):
                        pe.wait_ge(sem["att"], count(b, "att", c))
                out = ps[:, 4, (c % 2) * T:(c % 2) * T + T]
                if q == 0:
                    mm(out, ident[:], tok_fm[:, c, :], start=True, stop=False)
                for k in range(DH):
                    dd = q * DH + k
                    ins = mm(out, pick[:, HS - 1 - dd:HS - 1 - dd + P], S[:, u % 2, k, :],
                             start=False, stop=(dd == HS - 1))
                ins.then_inc(sem["red"], 1)

            def scores(a, i):
                qt, kv = divmod(i, KVH)
                if past(a, "neg", i - 1):
                    pe.wait_ge(sem["neg"], count(a, "neg", i - 1))
                for h in range(2):
                    ins = mm(tm["AB"[i % 2]][:, h, :], Q4[:, 2 * kv + h, qt * P:(qt + 1) * P],
                             K4[:, kv, :, :].rearrange("p a t -> p (a t)"), start=True, stop=True)
                ins.then_inc(sem["sc_ps"], 1)

            def turns(a, i):
                if 1 <= i <= AUNITS:
                    pe.wait_ge(sem["pr"], count(a, "pr", i))
                    if past(a, "pt", i - 1):
                        pe.wait_ge(sem["pt"], count(a, "pt", i - 1))
                    for t in range(2):
                        for h in range(GRP):
                            ins = nc.tensor.transpose(ps[:, 6 + t, h * P:(h + 1) * P],
                                                      SM[:, i % 2, h, t * P:(t + 1) * P], ident[:])
                    ins.then_inc(sem["pt_ps"], 1)
                if i >= 3 and (i - 3) % 4 == 3:
                    pe.wait_ge(sem["ot"], count(a, "ot", (i - 3) // 4 + 1))
                    for h in range(GRP):
                        ins = nc.tensor.transpose(ps[:, 5, h * P:(h + 1) * P], OT[:, h * P:(h + 1) * P], ident[:])
                    ins.then_inc(sem["ot_ps"], 1)

            def sums(a, i):
                if 2 <= i < AUNITS + 2:
                    kv = (i - 2) % KVH
                    pe.wait_ge(sem["pt"], count(a, "pt", i - 1))
                    if kv % 4 == 0:
                        if past(a, "ot2", (i - 2) // 4):
                            pe.wait_ge(sem["ot2"], count(a, "ot2", (i - 2) // 4))
                    at_ = 32 * (kv % 4)
                    for t in range(2):
                        ins = mm(ps[at_:at_ + 32, 5, :], vaug[:, t, kv, :], PT[:, t, :], start=(t == 0), stop=(t == 1))
                    ins.then_inc(sem["pv"], 1)

            def body(b, a):
                if b is not None:
                    before(b, a)
                else:
                    pe.wait_ge(sem["k4_in"], count(a, "k4_in", 128))
                    pe.wait_ge(sem["q4_in"], count(a, "q4_in", 128))
                    scores(a, 0)
                for i in range(STEPS):
                    if a is not None and i + 1 < AUNITS:
                        if b is not None and i == 0:
                            pe.wait_ge(sem["proj"], count(b, "proj", RS + 1))
                        scores(a, i + 1)
                    if b is not None and i == 1:
                        pe.wait_ge(sem["bonus"], count(b, "bonus", 1))
                    late = i > 3 and i % 4 == 2
                    if a is not None:
                        turns(a, i)
                        if not late:
                            sums(a, i)
                    if b is not None and i == 1:
                        pe.wait_ge(sem["gate"], count(b, "gate", 1))
                    if b is not None and 1 <= i <= UNITS:
                        reduce(b, i - 1)
                    if a is not None and late:
                        sums(a, i)
                    if b is not None and i == UNITS + 1:
                        pe.wait_ge(sem["att"], count(b, "att", C))
                        if a is not None:
                            pe.wait_ge(sem["neg"], count(a, "neg", AUNITS))
                        for tile in range(TT):
                            to_tokens(tm["A"], tok_fm, [tile]).then_inc(sem["att_ps"], 1)
                if b is not None:
                    pe.wait_ge(sem["ctx_in"], count(b, "ctx_in", 16))
                    for k in range(C):
                        ins = mm(ps[:, 2, 0:T], Wk1[:, k, :], rT[:, k, :], start=(k == 0), stop=(k == C - 1))
                    ins.then_inc(sem["k_ps"], 1)
                if a is not None:
                    pe.wait_ge(sem["at"], count(a, "at", SETS))
                    to_features(fm["C"], at).then_inc(sem["oT_ps"], 1)
                    pe.wait_ge(sem["oT"], count(a, "oT", 1))
                    tokens(tm["D"], xb, W["Wo1"], tiles=[0])
                if b is not None:
                    for i in range(TT):
                        pe.wait_ge(sem["cenr"], count(b, "cenr", i + 1))
                        ins = to_features(fm["A"], kT_tm, [i])
                    ins.then_inc(sem["aT_ps"], 1)
                    for i in range(TT):
                        for k in range(C):
                            ins = mm(ps[:, 3, i * P:(i + 1) * P], rT[:, k, i * P:(i + 1) * P], Wv1[:, k, :],
                                     start=(k == 0), stop=(k == C - 1))
                    ins.then_inc(sem["v_ps"], 1)
                    pe.wait_ge(sem["attg"], count(b, "attg", 1))
                    tokens(tm["C"], xa, W["WoT"], "wo_ps")
                    norm_to_features(b, 1, fm["A"])
                if a is not None:
                    tokens(tm["D"], xb, W["Wo1"], tiles=[1]).then_inc(sem["wo1_ps"], 1)
                if b is not None:
                    pe.wait_ge(sem["xk"], count(b, "xk", 1))
                    pe.wait_ge(sem["k_hi"], count(b, "k_hi", 1))
                    pe.wait_ge(sem["v_aug"], count(b, "v_aug", 1))
                    features(fm["B"], W["fWkT"], xa).then_inc(sem["kk_ps"], 1)
                    pe.wait_ge(sem["xr"], count(b, "xr", 1))
                    if a is not None:
                        pe.wait_ge(sem["y1"], count(a, "y1", 1))
                    tokens(tm["D"], xb, W["fWrT"]).then_inc(sem["rr_ps"], 1)
                    pe.wait_ge(sem["kk"], count(b, "kk", 1))
                    tokens(tm["C"], kT, W["fWvT"], "fv_ps")
                    for i in range(TT):
                        pe.wait_ge(sem["x2"], count(b, "x2", i + 1))
                        ins = to_features(fm["A"], res, [i])
                    ins.then_inc(sem["x2T_ps"], 1)
                    pe.wait_ge(sem["x2T"], count(b, "x2T", 1))
                    pe.wait_ge(sem["x2T_high"], count(b, "x2T_high", 1))
                    features(fm["D"], W["Wq"], xa).then_inc(sem["q_ps"], 1)

            iterate(pe, body)


def kernel(**inputs):
    import numpy as np
    import concourse.bacc as bacc
    from concourse.bass_utils import run_bass_kernel_spmd as run

    a = {n: np.asarray(v) for n, v in inputs.items()}
    L0, L1 = "L0_xattn_", "L1_xattn_"

    def chunks(w):
        return np.ascontiguousarray(w.reshape(C, P, -1).transpose(1, 0, 2))

    arrays = {
        "x": np.ascontiguousarray(a["x"].reshape(B, TT, P, E).transpose(0, 2, 1, 3)),
        "prev": np.ascontiguousarray(a["ctx_2048"][:, 0:2].reshape(B, 2, C, P).transpose(0, 3, 2, 1)),
        "ctxT": np.ascontiguousarray(a["ctx_2048"].reshape(B, T, C, P).transpose(0, 3, 2, 1)),
        "s0": np.ascontiguousarray(a["ctx_2048"][:, 2:2 + HS].reshape(B, C, P, HS).transpose(0, 2, 1, 3)),
        "mask": np.ascontiguousarray(a["mask_Bx1xSxS2_ff0"].reshape(B, TT, P, T).transpose(0, 2, 1, 3)),
        "mw1": chunks(a[L0 + "maa_w1"]),
        "dw1": chunks(a[L0 + "decay_w1"]),
        "dw2": np.concatenate([a[L0 + "decay_w2"], np.zeros((P - DEC, E), np.float32)]),
        "bv": a[L1 + "bv"],
        "bo": a[L1 + "bo"], "gamma": a[L1 + "gamma"], "beta": a[L1 + "beta"],
    }
    w2 = np.zeros((P, 2, E), np.float32)
    w2[:, 0] = a[L0 + "maa_w2"][0:4].reshape(P, E)
    w2[0:MAA, 1] = a[L0 + "maa_w2"][4]
    arrays["mw2"] = w2
    for n, k in (("WrT", "Wr"), ("WkT", "Wk"), ("WvT", "Wv"), ("WgT", "Wg"), ("WoT", "Wo"),
                 ("fWkT", "ffn_Wk"), ("fWrT", "ffn_Wr"), ("fWvT", "ffn_Wv")):
        arrays[n] = chunks(a[L0 + k].T)
    for n, k in (("Wq", "Wq"), ("Wk1", "Wk"), ("Wv1", "Wv"), ("Wo1", "Wo")):
        arrays[n] = chunks(a[L1 + k])
    flat = {"bq": a[L1 + "bq"], "faaaa": a[L0 + "faaaa"].reshape(E)}
    for s in range(5):
        flat[f"stack{s}"] = a[L0 + "maa_stack"][s]
    cols = [flat[n] if n in flat else a[L0 + n] for n in VECS]
    arrays["vec"] = np.ascontiguousarray(
        np.concatenate([v.reshape(C, P) for v in cols] + [a[L1 + "bk"].reshape(1, P)]).T)

    nc = bacc.Bacc("TRN2", target_bir_lowering=False, num_devices=1, dynamic_dma_scratch_size=2048)
    d = {n: nc.dram_tensor("in_" + n, v.shape, F32, kind="ExternalInput").ap() for n, v in arrays.items()}
    d["out"] = nc.dram_tensor("out_y", (B, P, TT, E), F32, kind="ExternalOutput").ap()
    build(nc, d)
    r = run(nc, [{"in_" + n: v for n, v in arrays.items()}], core_ids=[0])
    y = np.asarray(r.results[0]["out_y"])
    return np.ascontiguousarray(y.reshape(B, P, TT, E).transpose(0, 2, 1, 3).reshape(B, T, E))
```
